# Optimizing a Trainium2 kernel written in Bass

```python
import numpy as np
import jax
import jax.numpy as jnp

def _softmax(x, axis=-1):
    return jax.nn.softmax(x, axis=axis)

def _gelu(x):
    return jax.nn.gelu(x, approximate=True)

def _silu(x):
    return jax.nn.silu(x)

def _sigmoid(x):
    return jax.nn.sigmoid(x)

def _layernorm(x, axis=-1, eps=1e-05):
    m = jnp.mean(x, axis=axis, keepdims=True)
    v = jnp.var(x, axis=axis, keepdims=True)
    return (x - m) / jnp.sqrt(v + eps)

def _scatter_add(tgt, idx, src, axis=0):
    return tgt.at[idx].add(src)

def _segment_sum(src, seg, n):
    return jax.ops.segment_sum(src, seg, n)
kernel_name = 'mk_conv_seq_d1_conv_nchw512_r2_6f6ea7'

def setup_inputs(seed: int=0):
    np.random.seed(seed)
    _w = jnp.asarray

    def _rec_inputs():
        import jax
        import jax.numpy as jnp
        _gk = jax.random.key(seed)
        x = 7.22e-05 + 1 * jax.random.normal(jax.random.fold_in(_gk, 1), (4, 256, 32, 32), jnp.float32)
        return x
    x = _rec_inputs()

    def _L0_conv_setup():
        import jax, jax.numpy as jnp
        import numpy as np
        N_HEADS = 4
        N_GROUPS = 32
        EPS = 1e-05

        def _group_norm(x, w, b):
            bsz, c, h, wd = x.shape
            xg = x.reshape(bsz, N_GROUPS, c // N_GROUPS, h, wd)
            mean = xg.mean(axis=(2, 3, 4), keepdims=True)
            var = xg.var(axis=(2, 3, 4), keepdims=True)
            xg = (xg - mean) * jax.lax.rsqrt(var + EPS)
            x = xg.reshape(bsz, c, h, wd)
            return x * w[None, :, None, None] + b[None, :, None, None]

        def _conv1x1(x, w, b):
            return jnp.einsum('bchw,oc->bohw', x, w) + b[None, :, None, None]
        key = jax.random.key(seed)
        ks = jax.random.split(key, 6)
        c = 256
        x = jax.random.normal(ks[0], (4, c, 32, 32), dtype=jnp.float32)
        s = 1.0 / np.sqrt(c)
        wq = jax.random.normal(ks[1], (c, c), dtype=jnp.float32) * s
        wk = jax.random.normal(ks[2], (c, c), dtype=jnp.float32) * s
        wv = jax.random.normal(ks[3], (c, c), dtype=jnp.float32) * s
        wp = jax.random.normal(ks[4], (c, c), dtype=jnp.float32) * s
        zeros = jnp.zeros((c,), dtype=jnp.float32)
        return {'x': x, 'gn_w': jnp.ones((c,), dtype=jnp.float32), 'gn_b': zeros, 'wq': wq, 'bq': zeros, 'wk': wk, 'bk': zeros, 'wv': wv, 'bv': zeros, 'wp': wp, 'bp': zeros}
    _L0_conv_all = _L0_conv_setup()
    _L0_conv_in = {k: v for k, v in _L0_conv_all.items() if k in ('gn_w', 'gn_b', 'wq', 'bq', 'wk', 'bk', 'wv', 'bv', 'wp', 'bp')}
    del _L0_conv_all
    return {'x': x, 'L0_conv_gn_w': _L0_conv_in['gn_w'], 'L0_conv_gn_b': _L0_conv_in['gn_b'], 'L0_conv_wq': _L0_conv_in['wq'], 'L0_conv_bq': _L0_conv_in['bq'], 'L0_conv_wk': _L0_conv_in['wk'], 'L0_conv_bk': _L0_conv_in['bk'], 'L0_conv_wv': _L0_conv_in['wv'], 'L0_conv_bv': _L0_conv_in['bv'], 'L0_conv_wp': _L0_conv_in['wp'], 'L0_conv_bp': _L0_conv_in['bp']}

def reference(x, L0_conv_gn_w, L0_conv_gn_b, L0_conv_wq, L0_conv_bq, L0_conv_wk, L0_conv_bk, L0_conv_wv, L0_conv_bv, L0_conv_wp, L0_conv_bp):
    import jax
    import jax.numpy as jnp

    def _L0_conv_ref(x, gn_w, gn_b, wq, bq, wk, bk, wv, bv, wp, bp):
        import jax, jax.numpy as jnp
        import numpy as np
        N_HEADS = 4
        N_GROUPS = 32
        EPS = 1e-05

        def _group_norm(x, w, b):
            bsz, c, h, wd = x.shape
            xg = x.reshape(bsz, N_GROUPS, c // N_GROUPS, h, wd)
            mean = xg.mean(axis=(2, 3, 4), keepdims=True)
            var = xg.var(axis=(2, 3, 4), keepdims=True)
            xg = (xg - mean) * jax.lax.rsqrt(var + EPS)
            x = xg.reshape(bsz, c, h, wd)
            return x * w[None, :, None, None] + b[None, :, None, None]

        def _conv1x1(x, w, b):
            return jnp.einsum('bchw,oc->bohw', x, w) + b[None, :, None, None]
        bsz, c, h, wd = x.shape
        hd = c // N_HEADS
        hw = h * wd
        x_n = _group_norm(x, gn_w, gn_b)
        q = _conv1x1(x_n, wq, bq)
        k = _conv1x1(x_n, wk, bk)
        v = _conv1x1(x_n, wv, bv)

        def to_heads(t):
            return t.reshape(bsz, N_HEADS, hd, hw).transpose(0, 1, 3, 2)
        q, k, v = (to_heads(q), to_heads(k), to_heads(v))
        scale = hd ** (-0.5)
        attn = jnp.einsum('bhqd,bhkd->bhqk', q, k) * scale
        attn = jax.nn.softmax(attn, axis=-1)
        out = jnp.einsum('bhqk,bhkd->bhqd', attn, v)
        out = out.transpose(0, 1, 3, 2).reshape(bsz, c, h, wd)
        out = _conv1x1(out, wp, bp)
        return x + out

    def _gn(v, G=32, eps=1e-05):
        B_, C_, H_, W_ = v.shape
        g = v.reshape(B_, G, C_ // G, H_, W_)
        m = jnp.mean(g, axis=(2, 3, 4), keepdims=True)
        s = jnp.var(g, axis=(2, 3, 4), keepdims=True)
        return ((g - m) / jnp.sqrt(s + eps)).reshape(v.shape)

    def _ln_c(v, eps=1e-06):
        m = jnp.mean(v, axis=1, keepdims=True)
        s = jnp.var(v, axis=1, keepdims=True)
        return (v - m) / jnp.sqrt(s + eps)

    def _ln_t(v, eps=1e-05):
        m = jnp.mean(v, axis=-1, keepdims=True)
        s = jnp.var(v, axis=-1, keepdims=True)
        return (v - m) / jnp.sqrt(s + eps)

    def _to_tokens(v):
        B_, C_, H_, W_ = v.shape
        return v.reshape(B_, C_, H_ * W_).transpose(0, 2, 1)

    def _from_tokens(t, like):
        B_, C_, H_, W_ = like.shape
        return t.transpose(0, 2, 1).reshape(B_, C_, H_, W_)
    x = _L0_conv_ref(x, L0_conv_gn_w, L0_conv_gn_b, L0_conv_wq, L0_conv_bq, L0_conv_wk, L0_conv_bk, L0_conv_wv, L0_conv_bv, L0_conv_wp, L0_conv_bp)
    return x

_drawn_inputs = setup_inputs


def setup_inputs(seed=0):
    import zlib

    import numpy as np

    out = dict(_drawn_inputs(seed))
    spreads = {'L0_conv_gn_w': (1.0, 0.2),
     'L0_conv_gn_b': (0.0, 0.1),
     'L0_conv_bq': (0.0, 0.8),
     'L0_conv_bk': (0.0, 0.8),
     'L0_conv_bv': (0.0, 0.1),
     'L0_conv_bp': (0.0, 0.1)}
    factors = {}
    for name, (base, spread) in spreads.items():
        noise = np.random.default_rng([zlib.crc32(name.encode()), seed]).standard_normal(out[name].shape)
        drawn = base * np.exp(spread * noise) if base else spread * noise
        out[name] = jnp.asarray(drawn.astype(out[name].dtype))
    for name, factor in factors.items():
        out[name] = (out[name] * factor).astype(out[name].dtype)
    return out
```

```python
from contextlib import ExitStack

import concourse.bass as bass
from concourse import mybir

F32 = mybir.dt.float32
F16 = mybir.dt.float16
ALU = mybir.AluOpType
ACT = mybir.ActivationFunctionType
AX = mybir.AxisListType


def attention_block(nc, x, gn_w, gn_b, wq, bq, wk, bk, wv, bv, wp, bp, out):
    B, C, IH, IW = x.shape
    HW = IH * IW
    P = 128
    HEADS = 4
    D = C // HEADS
    GROUP = C // 32
    CT = C // P
    NK = HW // P
    HALF = HW // 2
    QT = HALF // P
    UNITS = HEADS * 2
    SPU = 4
    CPS = NK // SPU
    SLOTS = UNITS * SPU
    LAG = 3
    TURN = 10
    MXJ = 2 * QT + 1
    PR = 8
    PV = D + 1
    EPS = 1e-5
    OUT_SEED = 16

    Z_SCALE = 512.0
    W_SCALE = 1024.0
    QKV_SCALE = 32.0
    M_SCALE = QKV_SCALE * QKV_SCALE
    O_SCALE = 128.0
    P_LOG = 8.317766166719343
    SM_SCALE = D ** -0.5

    x_v = x.rearrange("b (t p) h w -> b p t (h w)", p=P)
    out_v = out.rearrange("b (t p) h w -> b p t (h w)", p=P)

    JOBS = {0: ("k", 1, 0, 0), 1: ("k", 1, 1, 0), 2: ("q", 1, 0, 0), 3: ("q", 1, 1, 0),
            4: ("o", 1, 1, -1), 5: ("y", 0, 0, -1), 6: ("y", 1, 0, -1), 7: ("y", 0, 1, -1), 8: ("y", 1, 1, -1),
            9: ("v", 1, 0, 0), 10: ("v", 1, 1, 0), 11: ("o", 0, 0, 0),
            14: ("mean", 0, 0, 1), 16: ("var", 0, 0, 1), 20: ("o", 0, 1, 0),
            21: ("k", 0, 0, 1), 22: ("k", 0, 1, 1), 23: ("q", 0, 0, 1), 24: ("q", 0, 1, 1),
            25: ("v", 0, 0, 1), 26: ("v", 0, 1, 1), 28: ("o", 1, 0, 0)}
    FIRST_JOBS = [("k", 0, 0), ("k", 0, 1), ("q", 0, 0), ("q", 0, 1), ("v", 0, 0), ("v", 0, 1)]
    SPLIT = ("k", "q", "v", "o")

    ctx = ExitStack()
    with ctx:
        def sb(name, shape, dt=F32):
            return ctx.enter_context(nc.sbuf_tensor(name, shape, dt))

        def sem(name):
            return ctx.enter_context(nc.semaphore(name))

        ident = sb("ident", [P, P])
        ident16 = sb("ident16", [P, P], F16)
        group_avg = sb("group_avg", [P, P])
        w_in = {n: sb(f"w_in_{n}", [P, CT, C]) for n in "kqvp"}
        wT = {n: sb(f"wT_{n}", [P, CT, C]) for n in "kqvp"}
        w_sc = {n: sb(f"w_sc_{n}", [P, CT, C]) for n in "kqvp"}
        w_hi = {n: sb(f"w_hi_{n}", [P, CT, C], F16) for n in "kqvp"}
        w_lo = {n: sb(f"w_lo_{n}", [P, CT, C], F16) for n in "kqvp"}
        vec_rows = sb("vec_rows", [6 * CT, P])
        vec_cols = sb("vec_cols", [P, 6 * CT])
        vec = {n: vec_cols[:, CT * m:CT * (m + 1)] for m, n in enumerate(("gn_w", "gn_b", "k", "q", "v", "p"))}
        gam_sc = sb("gam_sc", [P, CT])
        w_gnb = sb("w_gnb", [P, 3, CT])
        bias = {n: sb(f"bias_{n}", [P, CT]) for n in "kqvp"}
        bias_s = {n: sb(f"bias_s_{n}", [P, CT]) for n in "kq"}
        wp_bv = sb("wp_bv", [P, CT])
        xin = sb("xin", [P, CT, HW])
        bn = sb("bn", [P, CT, 2, 6])
        mv = sb("mv", [P, CT, 2])
        gmean = sb("gmean", [P, CT])
        dev = sb("dev", [P, CT])
        dev2 = sb("dev2", [P, CT])
        gvar = sb("gvar", [P, CT])
        veps = sb("veps", [P, CT])
        expo = sb("expo", [P, CT])
        eps = sb("eps", [P, CT])
        rstd = sb("rstd", [P, CT])
        z_a = sb("z_a", [P, CT])
        z_b = sb("z_b", [P, CT])
        z_hi = sb("z_hi", [P, CT, HW], F16)
        z_lo = sb("z_lo", [P, CT, HW], F16)
        e32 = {n: sb(f"e32_{n}", [P, 2, HALF]) for n in SPLIT}
        kq_hi = {n: sb(f"st_hi_{n}", [P, HW], F16) for n in "kq"}
        kq_lo = {n: sb(f"st_lo_{n}", [P, HW], F16) for n in "kq"}
        k_both = sb("k_both", [P, HEADS, HW], F16)
        q_twice = sb("q_twice", [P, HEADS, HW], F16)
        k_one = sb("k_one", [D + 1, HEADS, HW], F16)
        q_max = sb("q_max", [D + 1, HEADS, HW], F16)
        v_hi = sb("v_hi", [P, NK, HEADS, PV], F16)
        v_lo = sb("v_lo", [P, NK, HEADS, D], F16)
        mx8 = sb("mx8", [P, 2, QT, 2])
        mx4 = sb("mx4", [P, 2, QT])
        shift = sb("shift", [P, 2, QT], F16)
        shift_row = sb("shift_row", [QT, 2, P], F16)
        p32 = sb("p32", [P, SPU, CPS * HALF])
        p_hi = sb("p_hi", [P, PR, CPS, HALF], F16)
        p_lo = sb("p_lo", [P, PR, CPS, HALF], F16)
        rden = sb("rden", [P, 2, QT])
        o32 = sb("o32", [P, 2, QT, P])
        oT_hi = sb("oT_hi", [P, CT, HW], F16)
        oT_lo = sb("oT_lo", [P, CT, HW], F16)
        y32 = sb("y32", [P, 4, HALF])
        xres = sb("xres", [P, 4, HALF])

        def pb(name, n=1):
            return ctx.enter_context(nc.psum_tensor(name, [P, 512 * n], F32))

        st = [pb("st0", 2), pb("st1", 2)]
        mxb = [pb("mx0"), pb("mx1")]
        pv = pb("pv")
        gen = pb("gen")
        pv_v = pv[:, 0:QT * PV].rearrange("p (t n) -> p t n", n=PV)

        s_w = {n: sem(f"s_w_{n}") for n in "kqvp"}
        s_vec = sem("s_vec")
        s_xin = [sem(f"s_xin{t}") for t in range(CT)]
        s_xres = [sem(f"s_xres{j}") for j in range(4)]
        s_const = sem("s_const")
        s_cfill = sem("s_cfill")
        s_vecT = sem("s_vecT")
        s_cols = sem("s_cols")
        s_wT = sem("s_wT")
        s_gam = sem("s_gam")
        s_wraw = sem("s_wraw")
        s_wsc = sem("s_wsc")
        s_whi = sem("s_whi")
        s_wlo = sem("s_wlo")
        s_gnb = sem("s_gnb")
        s_bias = sem("s_bias")
        s_wpbv = sem("s_wpbv")
        s_mv = sem("s_mv")
        s_gmean = sem("s_gmean")
        s_dev = sem("s_dev")
        s_gvar = sem("s_gvar")
        s_ab = sem("s_ab")
        s_z32 = sem("s_z32")
        s_zhi = sem("s_zhi")
        s_zlo = sem("s_zlo")
        s_gen_full = sem("s_gen_full")
        s_e32 = {n: sem(f"s_e32_{n}") for n in SPLIT}
        s_hi = {n: sem(f"s_hi_{n}") for n in SPLIT}
        s_lo = {n: sem(f"s_lo_{n}") for n in SPLIT}
        s_dup = {n: sem(f"s_dup_{n}") for n in "kq"}
        s_mx_full = sem("s_mx_full")
        s_mx_free = sem("s_mx_free")
        s_shift = sem("s_shift")
        s_shift_dma = sem("s_shift_dma")
        s_st = sem("s_st")
        s_exp = sem("s_exp")
        s_phi = sem("s_phi")
        s_plo_dve = sem("s_plo_dve")
        s_plo_pool = sem("s_plo_pool")
        s_pv = sem("s_pv")
        s_o32 = sem("s_o32")
        s_y = sem("s_y")
        s_yx = sem("s_yx")
        s_out = sem("s_out")
        s_ones = sem("s_ones")

        block = ctx.enter_context(nc.Block())

        def count(b, per, k):
            reg, n = b
            return per * n + k if reg is None else reg * per + (per * n + k)

        def before(b):
            return b[0], b[1] - 1

        def after(b):
            return b[0], b[1] + 1

        def wait(eng, s, b, per, k):
            v = count(b, per, k)
            assert b[0] is None or per * b[1] + k > 0
            if b[0] is not None or v > 0:
                eng.wait_ge(s, v)

        class Tally:

            def __init__(self, per):
                self.n, self.per, self.turn, self.start = 0, per, None, 0

            def add(self):
                self.n += 1

            def value(self):
                return self.n if self.turn is None else self.turn * self.per + self.n

            def enter(self, turn):
                self.turn, self.start = turn, self.n

            def leave(self):
                assert self.n - self.start == self.per
                self.turn = None
                self.n += self.per * (B - 2)

        class Latest:

            def __init__(self):
                self.job = None

            def enter(self, turn):
                self.job = (*self.job[:3], (turn, self.job[3][1]))

            def leave(self):
                self.job = (*self.job[:3], (None, self.job[3][1] + B - 2))

        def batches(eng, slot, tallies=()):
            for g in range(TURN):
                slot((None, 0), g, False, True, True)
            with eng.Fori(0, B - 1) as turn:
                for t in tallies:
                    t.enter(turn)
                for g in range(TURN, SLOTS):
                    slot((turn, 0), g, True, True, True)
                for g in range(TURN):
                    slot((turn, 1), g, True, True, True)
                for t in tallies:
                    t.leave()
            for g in range(TURN, SLOTS):
                slot((None, B - 1), g, True, False, True)
            for g in range(TURN):
                slot((None, B), g, True, False, False)

        def job_at(g, b, prev, nxt, cur):
            if g not in JOBS:
                return None
            kind, i, j, rel = JOBS[g]
            if not {-1: prev, 0: cur, 1: nxt}[rel]:
                return None
            return kind, i, j, {-1: before(b), 0: b, 1: after(b)}[rel]

        def back(b, g, n, prev, cur):
            if g >= n:
                return (b, g - n) if cur else None
            return (before(b), g - n + SLOTS) if prev else None

        def next_unit(b, u, nxt, cur):
            if not cur:
                return None
            if u + 1 < UNITS:
                return b, u + 1
            return (after(b), 0) if nxt else None

        def unit(u):
            return 2 * (u // 4) + u % 2, (u // 2) % 2

        def lo_on_dve(g):
            return g % SPU in (1, 2)

        def wait_lo(eng, b, g):
            u, s = divmod(g, SPU)
            if lo_on_dve(g):
                wait(eng, s_plo_dve, b, 2 * UNITS, 2 * u + s)
            else:
                wait(eng, s_plo_pool, b, 2 * UNITS, 2 * u + (1 if s == 0 else 2))

        def v_parts(tile, i, j):
            return (tile[:, 4 * j:4 * j + 4, 2 * i:2 * i + 2, 0:D],
                    e32["v"][:, j, :].rearrange("p (c h d) -> p c h d", c=4, h=2))

        @block.sync
        def _(sp):
            sp.sem_inc(s_out, OUT_SEED)
            for t in range(CT):
                sp.dma_start(xin[:, t, :], x_v[0, :, t, :]).then_inc(s_xin[t], 16)
            for n, w in (("v", wv), ("p", wp)):
                sp.dma_start(w_in[n][:, :, :], w.rearrange("(t p) c -> p t c", p=P)).then_inc(s_w[n], 16)

            def dup(n, p, b):
                wait(sp, s_lo[n], b, 4, 2 * p + 2)
                heads = slice(2 * p, 2 * p + 2)
                top, low = (k_both, k_one) if n == "k" else (q_twice, q_max)
                for dst, src in ((top[0:D, heads, :], kq_hi[n]),
                                 (top[D:P, heads, :], kq_lo[n] if n == "k" else kq_hi[n]),
                                 (low[0:D, heads, :], kq_hi[n] if n == "k" else kq_lo[n])):
                    for h in range(2):
                        sp.dma_start(dst[:, h, :], src[h * D:(h + 1) * D, :]).then_inc(s_dup[n], 16)

            def shift_to_row(b, u):
                head, half = unit(u)
                wait(sp, s_mx_free, b, MXJ * UNITS, MXJ * (u + 1))
                sp.dma_start(q_max[D:D + 1, head, half * HALF:(half + 1) * HALF],
                             shift_row[:, u % 2, :]).then_inc(s_shift_dma, 16)

            def slot(b, g, prev, nxt, cur):
                u, s = divmod(g, SPU)
                if g == 1 and prev:
                    for j in range(4):
                        i, half = j % 2, j // 2
                        bb = before(b)
                        img = bb[1] if bb[0] is None else bb[0] + bb[1]
                        sp.dma_start(xres[:, j, :], x_v[img, :, i, half * HALF:(half + 1) * HALF])\
                          .then_inc(s_xres[j], 16)
                if g == 3 and cur:
                    dup("k", 1, b)
                if g == 5 and cur:
                    dup("q", 1, b)
                if g in (6, 7, 8, 9) and prev:
                    j = g - 6
                    wait(sp, s_yx, before(b), 4, j + 1)
                    bb = before(b)
                    img = bb[1] if bb[0] is None else bb[0] + bb[1]
                    i, half = j % 2, j // 2
                    sp.dma_start(out_v[img, :, i, half * HALF:(half + 1) * HALF], y32[:, j, :]).then_inc(s_out, 16)
                if g == TURN and nxt:
                    wait(sp, s_zlo, b, CT, CT)
                    bb = after(b)
                    img = bb[1] if bb[0] is None else bb[0] + bb[1]
                    for t in range(CT):
                        sp.dma_start(xin[:, t, :], x_v[img, :, t, :]).then_inc(s_xin[t], 16)
                if g == 24 and nxt:
                    dup("k", 0, after(b))
                if g == 26 and nxt:
                    dup("q", 0, after(b))
                if s == 2:
                    v = next_unit(b, u, nxt, cur)
                    if v:
                        shift_to_row(*v)

            dup("k", 0, (None, 0))
            dup("q", 0, (None, 0))
            shift_to_row((None, 0), 0)
            batches(sp, slot)
            sp.wait_ge(s_out, 16 * 4 * B + OUT_SEED)

        @block.tensor
        def _(pe):
            latest = Latest()

            def bank_empty():
                if latest.job is None:
                    return
                kind, i, j, b = latest.job
                if kind in SPLIT:
                    wait(pe, s_e32[kind], b, 4, 2 * i + j + 1)
                elif kind == "y":
                    wait(pe, s_y, b, 4, i + 2 * j + 1)
                else:
                    wait(pe, {"mean": s_gmean, "var": s_gvar, "gnb": s_gnb, "wpbv": s_wpbv}[kind], b, 1, 1)

            def parts(dst, lhs, rhs, first=True):
                for t in range(CT):
                    (lh, ll), (rh, rl) = lhs(t), rhs(t)
                    for n, (a, c) in enumerate(((lh, rh), (lh, rl), (ll, rh))):
                        yield nc.tensor.matmul(dst, a, c, start=first and t == 0 and n == 0,
                                               stop=t == CT - 1 and n == 2, skip_group_check=True)

            def job(kind, i, j, b):
                if kind in "kqv":
                    wait(pe, s_zlo, b, CT, CT)
                if kind == "mean":
                    wait(pe, s_mv, b, 1, 1)
                if kind == "var":
                    wait(pe, s_dev, b, 1, 1)
                if kind == "o":
                    wait(pe, s_o32, b, UNITS, 4 * i + 2 * j + 2)
                if kind == "y":
                    wait(pe, s_lo["o"], b, 4, 3 + j)
                bank_empty()
                half = slice(j * HALF, (j + 1) * HALF)
                if kind in "kq":
                    o = slice(i * P, (i + 1) * P)
                    for mm in parts(gen[:, :], lambda t: (w_hi[kind][:, t, o], w_lo[kind][:, t, o]),
                                    lambda t: (z_hi[:, t, half], z_lo[:, t, half])):
                        last = mm
                if kind == "v":
                    o = slice(i * P, (i + 1) * P)
                    for c in range(4):
                        k = slice((4 * j + c) * P, (4 * j + c + 1) * P)
                        for mm in parts(gen[:, c * P:(c + 1) * P], lambda t: (z_hi[:, t, k], z_lo[:, t, k]),
                                        lambda t: (w_hi["v"][:, t, o], w_lo["v"][:, t, o]), first=c == 0):
                            last = mm
                if kind == "y":
                    o = slice(i * P, (i + 1) * P)
                    for mm in parts(gen[:, :], lambda t: (w_hi["p"][:, t, o], w_lo["p"][:, t, o]),
                                    lambda t: (oT_hi[:, t, half], oT_lo[:, t, half])):
                        last = mm
                if kind == "o":
                    for q in range(QT):
                        last = nc.tensor.transpose(gen[:, q * P:(q + 1) * P], o32[:, j, q, :], ident[:, :])
                if kind == "mean":
                    last = nc.tensor.matmul(gen[:, 0:CT], group_avg[:, :], mv[:, :, 0], start=True, stop=True)
                if kind == "var":
                    last = nc.tensor.matmul(gen[:, 0:CT], group_avg[:, :], dev2[:, :], start=True, stop=True)
                last.then_inc(s_gen_full, 1)
                latest.job = (kind, i, j, b)

            def maximum(b, u, j):
                head, half = unit(u)
                wait(pe, s_mx_free, b, MXJ * UNITS, MXJ * u + j - 1)
                q = half * HALF + (j // 2) * P
                nc.tensor.matmul(mxb[(MXJ * u + j) % 2][:, :], q_twice[:, head, q:q + P],
                                 k_both[:, head, (j % 2) * 512:(j % 2 + 1) * 512],
                                 start=True, stop=True).then_inc(s_mx_full, 1)

            def shift_transpose(b, u):
                j = MXJ - 1
                wait(pe, s_mx_free, b, MXJ * UNITS, MXJ * u + j - 1)
                wait(pe, s_shift, b, UNITS, u + 1)
                nc.tensor.matmul(mxb[(MXJ * u + j) % 2][0:QT, 0:P], shift[:, u % 2, :], ident16[:, :],
                                 start=True, stop=True).then_inc(s_mx_full, 1)

            def scores(b, g):
                u, s = divmod(g, SPU)
                head, half = unit(u)
                q = slice(half * HALF, (half + 1) * HALF)
                if s == 0:
                    wait(pe, s_shift_dma, b, 16 * UNITS, 16 * (u + 1))
                wait(pe, s_exp, b, SLOTS, g - 1)
                for c in range(CPS):
                    k = slice((CPS * s + c) * P, (CPS * s + c + 1) * P)
                    dst = st[g % 2][:, c * HALF:(c + 1) * HALF]
                    nc.tensor.matmul(dst, k_both[:, head, k], q_twice[:, head, q], start=True, stop=False)
                    last = nc.tensor.matmul(dst, k_one[:, head, k], q_max[:, head, q], start=False, stop=True)
                last.then_inc(s_st, 1)

            def weigh(b, g):
                u, s = divmod(g, SPU)
                head, _ = unit(u)
                wait(pe, s_phi, b, SLOTS, g + 1)
                wait_lo(pe, b, g)
                if s == 0:
                    wait(pe, s_o32, b, UNITS, u)
                    if u % 4 == 0:
                        wait(pe, s_lo["v"], b, 4, u // 2 + 2)
                for c in range(CPS):
                    k = CPS * s + c
                    for q in range(QT):
                        qs = slice(q * P, (q + 1) * P)
                        hi, lo = p_hi[:, g % PR, c, qs], p_lo[:, g % PR, c, qs]
                        nc.tensor.matmul(pv_v[:, q, :], hi, v_hi[:, k, head, :], start=k == 0 and q == 0,
                                         stop=False, skip_group_check=True)
                        nc.tensor.matmul(pv_v[:, q, 0:D], hi, v_lo[:, k, head, :], start=False, stop=False,
                                         skip_group_check=True)
                        last = nc.tensor.matmul(pv_v[:, q, :], lo, v_hi[:, k, head, :], start=False,
                                                stop=k == NK - 1, skip_group_check=True)
                last.then_inc(s_pv, 1)

            def slot(b, g, prev, nxt, cur):
                u, s = divmod(g, SPU)
                v = next_unit(b, u, nxt, cur)
                if v and s == 0 and v[1] % 4 == 0:
                    for n in "kq":
                        wait(pe, s_dup[n], v[0], 16 * 12, 16 * 6 * (v[1] // 4 + 1))
                if cur:
                    scores(b, g)
                if v and s in (0, 1):
                    maximum(*v, 4 * s)
                    maximum(*v, 4 * s + 1)
                if v and s == 2:
                    shift_transpose(*v)
                todo = job_at(g, b, prev, nxt, cur)
                if todo:
                    job(*todo)
                if v and s in (0, 1):
                    maximum(*v, 4 * s + 2)
                    maximum(*v, 4 * s + 3)
                old = back(b, g, LAG, prev, cur)
                if old:
                    weigh(*old)

            pe.wait_ge(s_const, 3)
            pe.wait_ge(s_vec, 16 * 6)
            nc.tensor.transpose(pv[:, 0:6 * CT], vec_rows[:, :], ident[0:6 * CT, 0:6 * CT]).then_inc(s_vecT, 1)
            for m, n in enumerate("kqvp"):
                pe.wait_ge(s_w[n], 16)
                for t in range(CT):
                    for o in range(CT):
                        last = nc.tensor.transpose(st[m // 2][:, (m % 2) * 512 + t * C + o * P:][:, 0:P],
                                                   w_in[n][:, o, t * P:(t + 1) * P], ident[:, :])
                last.then_inc(s_wT, 1)
            job("mean", 0, 0, (None, 0))
            pe.wait_ge(s_wraw, 3)
            pe.wait_ge(s_cols, 1)
            bank_empty()
            for m, n in enumerate("kqv"):
                for o in range(CT):
                    for t in range(CT):
                        last = nc.tensor.matmul(gen[:, m * CT + o:m * CT + o + 1], wT[n][:, t, o * P:(o + 1) * P],
                                                vec["gn_b"][:, t:t + 1], start=m == o == t == 0, stop=t == CT - 1,
                                                skip_group_check=True)
            last.then_inc(s_gen_full, 1)
            latest.job = ("gnb", 0, 0, (None, 0))
            job("var", 0, 0, (None, 0))
            pe.wait_ge(s_wlo, 3)
            for kind, i, j in FIRST_JOBS:
                job(kind, i, j, (None, 0))
            pe.wait_ge(s_bias, 3)
            pe.wait_ge(s_wlo, 4)
            bank_empty()
            for o in range(CT):
                for t in range(CT):
                    last = nc.tensor.matmul(gen[:, o:o + 1], wT["p"][:, t, o * P:(o + 1) * P],
                                            bias["v"][:, t:t + 1], start=o == t == 0, stop=t == CT - 1,
                                            skip_group_check=True)
            last.then_inc(s_gen_full, 1)
            latest.job = ("wpbv", 0, 0, (None, 0))
            for n in "kq":
                pe.wait_ge(s_dup[n], 16 * 6)
            pe.wait_ge(s_ones, 2)
            for j in range(MXJ - 1):
                maximum((None, 0), 0, j)
            shift_transpose((None, 0), 0)
            batches(pe, slot, [latest])

        @block.scalar
        def _(act):
            jobs = Tally(len(JOBS))

            for n, w in (("k", wk), ("q", wq)):
                act.dma_start(w_in[n][:, :, :], w.rearrange("(t p) c -> p t c", p=P)).then_inc(s_w[n], 16)
            for m, a in enumerate((gn_w, gn_b, bk, bq, bv, bp)):
                act.dma_start(vec_rows[CT * m:CT * (m + 1), :], a.rearrange("(t p) -> t p", p=P)).then_inc(s_vec, 16)

            def job(kind, i, j, b):
                jobs.add()
                act.wait_ge(s_gen_full, jobs.value())
                if kind in SPLIT and not (kind == "o" and i == 0):
                    wait(act, s_lo[kind], b, 4, max(2 * i + j - 1, 0))
                if kind in "kq":
                    last = nc.scalar.activation(e32[kind][:, j, :], gen[:, :], ACT.Identity,
                                                bias=bias_s[kind][:, i:i + 1],
                                                scale=QKV_SCALE / (Z_SCALE * W_SCALE))
                if kind == "v":
                    last = nc.scalar.activation(e32[kind][:, j, :], gen[:, :], ACT.Copy,
                                                scale=QKV_SCALE / (Z_SCALE * W_SCALE))
                if kind == "o":
                    last = nc.scalar.activation(e32[kind][:, j, :], gen[:, :], ACT.Copy, scale=O_SCALE)
                if kind in SPLIT:
                    last.then_inc(s_e32[kind], 1)
                if kind == "y":
                    wait(act, s_out, b, 64, OUT_SEED)
                    last = nc.scalar.activation(y32[:, i + 2 * j, :], gen[:, :], ACT.Identity,
                                                bias=bias["p"][:, i:i + 1], scale=1.0 / (O_SCALE * W_SCALE))
                    last.then_inc(s_y, 1)
                if kind == "mean":
                    nc.scalar.activation(gmean[:, :], gen[:, 0:CT], ACT.Copy).then_inc(s_gmean, 1)
                if kind == "var":
                    nc.scalar.activation(gvar[:, :], gen[:, 0:CT], ACT.Copy).then_inc(s_gvar, 1)

            def slot(b, g, prev, nxt, cur):
                u, s = divmod(g, SPU)
                if cur:
                    wait(act, s_st, b, SLOTS, g + 1)
                    if g >= SPU or prev:
                        wait_lo(act, *back(b, g, SPU, prev, cur))
                    nc.scalar.activation(p32[:, s, :], st[g % 2][:, :], ACT.Exp, scale=SM_SCALE / M_SCALE)\
                      .then_inc(s_exp, 1)
                todo = job_at(g, b, prev, nxt, cur)
                if todo:
                    job(*todo)
                if g in (18, 19) and nxt:
                    z_high(after(b), g - 18)
                if cur:
                    wait(act, s_exp, b, SLOTS, g + 1)
                    wait(act, s_pv, b, SLOTS, g + 1 - PR)
                    nc.scalar.activation(p_hi[:, g % PR, :, :], p32[:, s, :].rearrange("p (c n) -> p c n", n=HALF),
                                         ACT.Copy).then_inc(s_phi, 1)

            def z_high(b, t):
                wait(act, s_z32, b, CT, t + 1)
                nc.scalar.activation(z_hi[:, t, :], xin[:, t, :], ACT.Copy).then_inc(s_zhi, 1)

            def from_bank(dst, signal):
                jobs.add()
                act.wait_ge(s_gen_full, jobs.value())
                nc.scalar.activation(dst, gen[:, 0:dst.free_size()], ACT.Copy).then_inc(signal, 1)

            act.wait_ge(s_gam, 1)
            for m, n in enumerate("kqvp"):
                act.wait_ge(s_wT, m + 1)
                src = st[m // 2][:, (m % 2) * 512:(m % 2 + 1) * 512].rearrange("p (t o) -> p t o", t=CT)
                nc.scalar.activation(wT[n][:, :, :], src, ACT.Copy).then_inc(s_wraw, 1)
                for t in range(CT):
                    scale = W_SCALE if n == "p" else gam_sc[:, t:t + 1]
                    nc.scalar.activation(w_sc[n][:, t, :], src[:, t, :], ACT.Copy, scale=scale).then_inc(s_wsc, 1)
                act.wait_ge(s_wsc, CT * (m + 1))
                nc.scalar.activation(w_hi[n][:, :, :], w_sc[n][:, :, :], ACT.Copy).then_inc(s_whi, 1)
            job("mean", 0, 0, (None, 0))
            from_bank(w_gnb[:, :, :].rearrange("p n o -> p (n o)"), s_gnb)
            job("var", 0, 0, (None, 0))
            z_high((None, 0), 0)
            z_high((None, 0), 1)
            act.wait_ge(s_bias, 2)
            for kind, i, j in FIRST_JOBS:
                job(kind, i, j, (None, 0))
            from_bank(wp_bv[:, :], s_wpbv)
            act.wait_ge(s_bias, 4)
            batches(act, slot, [jobs])

        @block.vector
        def _(dve):
            def then(ins):
                dve.drain()

            def row_max(b, u, j):
                wait(dve, s_mx_full, b, MXJ * UNITS, MXJ * u + j + 1)
                nc.vector.reduce_max(mx8[:, u % 2, j // 2, j % 2:j % 2 + 1], mxb[(MXJ * u + j) % 2][:, :], AX.X)\
                  .then_inc(s_mx_free, 1)

            def make_shift(b, u):
                wait(dve, s_mx_free, b, MXJ * UNITS, MXJ * u + 2 * QT)
                then(nc.vector.reduce_max(mx4[:, u % 2, :], mx8[:, u % 2, :, :], AX.X))
                nc.vector.tensor_scalar(shift[:, u % 2, :], mx4[:, u % 2, :], -1.0 / M_SCALE, P_LOG / SM_SCALE,
                                        ALU.mult, ALU.add).then_inc(s_shift, 1)

            def row_out(b, u):
                wait(dve, s_mx_full, b, MXJ * UNITS, MXJ * (u + 1))
                wait(dve, s_shift_dma, b, 16 * UNITS, 16 * (u - 1))
                nc.vector.tensor_copy(shift_row[:, u % 2, :], mxb[(MXJ * u + MXJ - 1) % 2][0:QT, 0:P])\
                  .then_inc(s_mx_free, 1)

            def high(kind, i, j, b):
                wait(dve, s_e32[kind], b, 4, 2 * i + j + 1)
                half = slice(j * HALF, (j + 1) * HALF)
                src = e32[kind][:, j, :]
                if kind in "kq":
                    wait(dve, s_dup[kind], b, 16 * 12, 16 * 6 * i)
                    dst = kq_hi[kind][:, half]
                if kind == "v":
                    dst, src = v_parts(v_hi, i, j)
                if kind == "o":
                    dst = oT_hi[:, i, half]
                nc.vector.tensor_copy(dst, src).then_inc(s_hi[kind], 1)

            def normalise(b, u):
                head, half = unit(u)
                wait(dve, s_pv, b, SLOTS, SPU * (u + 1))
                then(nc.vector.reciprocal(rden[:, u % 2, :], pv_v[:, :, D]))
                nc.vector.tensor_tensor(o32[:, half, :, (u % 2) * D:(u % 2 + 1) * D], pv_v[:, :, 0:D],
                                        rden[:, u % 2, :].unsqueeze(2).to_broadcast([P, QT, D]), ALU.mult)\
                  .then_inc(s_o32, 1)

            def channel_stats(b, t):
                wait(dve, s_xin[t], b, 16, 16)
                for n in range(2):
                    then(nc.vector.bn_stats(bn[:, t, n, :], xin[:, t, n * 512:(n + 1) * 512]))
                ins = nc.vector.bn_aggr(mv[:, t, :], bn[:, t, :, :].rearrange("p n s -> p (n s)"))
                if t == CT - 1:
                    ins.then_inc(s_mv, 1)

            def about_group_mean(b):
                wait(dve, s_gmean, b, 1, 1)
                wait(dve, s_mv, b, 1, 1)
                then(nc.vector.tensor_tensor(dev[:, :], mv[:, :, 0], gmean[:, :], ALU.subtract))
                then(nc.vector.tensor_tensor(dev[:, :], dev[:, :], dev[:, :], ALU.mult))
                nc.vector.tensor_tensor(dev2[:, :], dev[:, :], mv[:, :, 1], ALU.add).then_inc(s_dev, 1)

            def z_of(b, t):
                wait(dve, s_ab, b, 1, 1)
                nc.vector.tensor_scalar(xin[:, t, :], xin[:, t, :], z_a[:, t:t + 1], z_b[:, t:t + 1],
                                        ALU.mult, ALU.add).then_inc(s_z32, 1)

            def slot(b, g, prev, nxt, cur):
                u, s = divmod(g, SPU)
                v = next_unit(b, u, nxt, cur)
                if s == 3:
                    old = back(b, g, SPU, prev, cur)
                    if old:
                        normalise(old[0], old[1] // SPU)
                if v and s in (0, 1):
                    row_max(*v, 4 * s)
                    row_max(*v, 4 * s + 1)
                if v and s == 2:
                    row_out(*v)
                old = back(b, g, 1, prev, cur)
                if old and lo_on_dve(old[1]):
                    wait(dve, s_phi, old[0], SLOTS, old[1] + 1)
                    nc.vector.tensor_tensor(p_lo[:, old[1] % PR, :, :],
                                            p32[:, old[1] % SPU, :].rearrange("p (c n) -> p c n", n=HALF),
                                            p_hi[:, old[1] % PR, :, :], ALU.subtract).then_inc(s_plo_dve, 1)
                if v and s in (0, 1):
                    row_max(*v, 4 * s + 2)
                    row_max(*v, 4 * s + 3)
                if v and s == 1:
                    make_shift(*v)
                if g in (12, 13) and nxt:
                    channel_stats(after(b), g - 12)
                if g == 15 and nxt:
                    about_group_mean(after(b))
                if g == 18 and nxt:
                    for t in range(CT):
                        z_of(after(b), t)
                todo = job_at(g - 1, b, prev, nxt, cur)
                if todo and todo[0] in SPLIT:
                    high(*todo)

            nc.vector.memset(k_one[D:D + 1, :, :], M_SCALE).then_inc(s_ones, 1)
            nc.vector.memset(v_hi[:, :, :, D], QKV_SCALE).then_inc(s_ones, 1)
            dve.wait_ge(s_vecT, 1)
            nc.vector.tensor_copy(vec_cols[:, :], pv[:, 0:6 * CT]).then_inc(s_cols, 1)
            dve.wait_ge(s_cols, 1)
            nc.vector.tensor_scalar(gam_sc[:, :], vec["gn_w"], W_SCALE, None, ALU.mult).then_inc(s_gam, 1)
            for t in range(CT):
                channel_stats((None, 0), t)
            about_group_mean((None, 0))
            dve.wait_ge(s_gnb, 1)
            for m, n in enumerate("kqv"):
                ins = nc.vector.tensor_tensor(bias[n][:, :], w_gnb[:, m, :], vec[n], ALU.add)
                if n == "v":
                    ins.then_inc(s_bias, 1)
                else:
                    then(ins)
                    nc.vector.tensor_scalar(bias_s[n][:, :], bias[n][:, :], QKV_SCALE, None, ALU.mult)\
                      .then_inc(s_bias, 1)
            for t in range(CT):
                z_of((None, 0), t)
            for kind, i, j in FIRST_JOBS:
                high(kind, i, j, (None, 0))
            dve.wait_ge(s_wpbv, 1)
            nc.vector.tensor_tensor(bias["p"][:, :], wp_bv[:, :], vec["p"], ALU.add).then_inc(s_bias, 1)
            for j in range(MXJ - 1):
                row_max((None, 0), 0, j)
            make_shift((None, 0), 0)
            row_out((None, 0), 0)
            batches(dve, slot)

        @block.gpsimd
        def _(pool):
            def then(ins):
                pool.drain()

            def low(kind, i, j, b):
                wait(pool, s_hi[kind], b, 4, 2 * i + j + 1)
                half = slice(j * HALF, (j + 1) * HALF)
                src = e32[kind][:, j, :]
                if kind in "kq":
                    hi, lo = kq_hi[kind][:, half], kq_lo[kind][:, half]
                if kind == "v":
                    (hi, src), (lo, _) = v_parts(v_hi, i, j), v_parts(v_lo, i, j)
                if kind == "o":
                    hi, lo = oT_hi[:, i, half], oT_lo[:, i, half]
                nc.gpsimd.tensor_tensor(lo, src, hi, ALU.subtract).then_inc(s_lo[kind], 1)

            def residual(i, half, b):
                j = i + 2 * half
                wait(pool, s_y, b, 4, j + 1)
                wait(pool, s_xres[j], b, 16, 16)
                nc.gpsimd.tensor_tensor(y32[:, j, :], y32[:, j, :], xres[:, j, :], ALU.add).then_inc(s_yx, 1)

            def norm_factors(b):
                wait(pool, s_gvar, b, 1, 1)
                wait(pool, s_gmean, b, 1, 1)
                then(nc.gpsimd.tensor_tensor(veps[:, :], gvar[:, :], eps[:, :], ALU.add))
                then(nc.gpsimd.tensor_tensor(rstd[:, :], veps[:, :], expo[:, :], ALU.pow))
                then(nc.gpsimd.tensor_tensor(z_a[:, :], rstd[:, :], rstd[:, :], ALU.mult))
                then(nc.gpsimd.tensor_tensor(z_a[:, :], z_a[:, :], veps[:, :], ALU.mult))
                then(nc.gpsimd.tensor_scalar(z_a[:, :], z_a[:, :], -0.5, 1.5, ALU.mult, ALU.add))
                then(nc.gpsimd.tensor_tensor(rstd[:, :], z_a[:, :], rstd[:, :], ALU.mult))
                then(nc.gpsimd.tensor_scalar(z_a[:, :], rstd[:, :], Z_SCALE, 0.0, ALU.mult, ALU.add))
                then(nc.gpsimd.tensor_tensor(z_b[:, :], z_a[:, :], gmean[:, :], ALU.mult))
                nc.gpsimd.tensor_scalar(z_b[:, :], z_b[:, :], -1.0, 0.0, ALU.mult, ALU.add).then_inc(s_ab, 1)

            def z_low(b, t):
                wait(pool, s_zhi, b, CT, t + 1)
                nc.gpsimd.tensor_tensor(z_lo[:, t, :], xin[:, t, :], z_hi[:, t, :], ALU.subtract).then_inc(s_zlo, 1)

            def slot(b, g, prev, nxt, cur):
                old = back(b, g, 1, prev, cur)
                if old and not lo_on_dve(old[1]):
                    wait(pool, s_phi, old[0], SLOTS, old[1] + 1)
                    nc.gpsimd.tensor_tensor(p_lo[:, old[1] % PR, :, :],
                                            p32[:, old[1] % SPU, :].rearrange("p (c n) -> p c n", n=HALF),
                                            p_hi[:, old[1] % PR, :, :], ALU.subtract).then_inc(s_plo_pool, 1)
                if g == 17 and nxt:
                    norm_factors(after(b))
                if g in (19, 20) and nxt:
                    z_low(after(b), g - 19)
                todo = job_at(g - 1, b, prev, nxt, cur)
                if todo and todo[0] in SPLIT:
                    low(*todo)
                if todo and todo[0] == "y":
                    residual(*todo[1:])

            nc.gpsimd.memset(ident[:, :], 0.0).then_inc(s_cfill, 1)
            nc.gpsimd.memset(ident16[:, :], 0.0).then_inc(s_cfill, 1)
            nc.gpsimd.memset(group_avg[:, :], 1.0 / GROUP).then_inc(s_cfill, 1)
            nc.gpsimd.memset(expo[:, :], -0.5).then_inc(s_cfill, 1)
            nc.gpsimd.memset(eps[:, :], EPS).then_inc(s_cfill, 1)
            pool.wait_ge(s_cfill, 5)
            for m in (ident, ident16):
                nc.gpsimd.affine_select(out=m[:, :], in_=m[:, :], compare_op=ALU.not_equal, fill=1.0, base=0,
                                        pattern=[[-1, P]], channel_multiplier=1).then_inc(s_const, 1)
            blocks = group_avg[:, :].rearrange("p (g n) -> p g n", n=GROUP)
            then(nc.gpsimd.affine_select(out=blocks, in_=blocks, compare_op=ALU.is_ge, fill=0.0, base=0,
                                         pattern=[[-GROUP, P // GROUP], [0, GROUP]], channel_multiplier=1))
            nc.gpsimd.affine_select(out=blocks, in_=blocks, compare_op=ALU.is_ge, fill=0.0, base=GROUP - 1,
                                    pattern=[[GROUP, P // GROUP], [0, GROUP]], channel_multiplier=-1)\
              .then_inc(s_const, 1)
            for m, n in enumerate("kqvp"):
                pool.wait_ge(s_whi, m + 1)
                nc.gpsimd.tensor_tensor(w_lo[n][:, :, :], w_sc[n][:, :, :], w_hi[n][:, :, :], ALU.subtract)\
                  .then_inc(s_wlo, 1)
            norm_factors((None, 0))
            for t in range(CT):
                z_low((None, 0), t)
            for kind, i, j in FIRST_JOBS:
                low(kind, i, j, (None, 0))
            batches(pool, slot)


_INS = ["x", "L0_conv_gn_w", "L0_conv_gn_b", "L0_conv_wq", "L0_conv_bq", "L0_conv_wk", "L0_conv_bk",
        "L0_conv_wv", "L0_conv_bv", "L0_conv_wp", "L0_conv_bp"]


def kernel(**inputs):
    import numpy as _np
    import concourse.bacc as _bacc
    from concourse import mybir as _mybir
    from concourse.bass_utils import run_bass_kernel_spmd as _run

    nc = _bacc.Bacc("TRN2", target_bir_lowering=False, num_devices=1)
    arrays, args = {}, []
    for name in _INS:
        a = _np.ascontiguousarray(inputs[name])
        arrays[f"in_{name}_dram"] = a
        args.append(nc.dram_tensor(f"in_{name}_dram", a.shape, _mybir.dt.from_np(a.dtype), kind="ExternalInput").ap())
    shape = inputs["x"].shape
    args.append(nc.dram_tensor("out_0_dram", shape, _mybir.dt.float32, kind="ExternalOutput").ap())
    attention_block(nc, *args)
    r = _run(nc, [arrays], core_ids=[0])
    return r.results[0]["out_0_dram"]
```

```python
from contextlib import ExitStack

import concourse.bass as bass
from concourse import mybir

F32 = mybir.dt.float32
F16 = mybir.dt.float16
ALU = mybir.AluOpType
ACT = mybir.ActivationFunctionType
AX = mybir.AxisListType


def attention_block(nc, x, gn_w, gn_b, wq, bq, wk, bk, wv, bv, wp, bp, out):
    B, C, IH, IW = x.shape
    HW = IH * IW
    P = 128
    HEADS = 4
    D = C // HEADS
    GROUP = C // 32
    CT = C // P
    NK = HW // P
    HALF = HW // 2
    QT = HALF // P
    UNITS = HEADS * 2
    SPU = 4
    CPS = NK // SPU
    SLOTS = UNITS * SPU
    LAG = 4
    TURN = 10
    MX_AHEAD = 6
    MXJ = 2 * QT + 1
    PR = 8
    PV = D + 1
    EPS = 1e-5
    OUT_SEED = 16

    Z_SCALE = 512.0
    W_SCALE = 1024.0
    QKV_SCALE = 32.0
    M_SCALE = QKV_SCALE * QKV_SCALE
    O_SCALE = 128.0
    P_LOG = 8.317766166719343
    SM_SCALE = D ** -0.5

    x_v = x.rearrange("b (t p) h w -> b p t (h w)", p=P)
    out_v = out.rearrange("b (t p) h w -> b p t (h w)", p=P)

    JOBS = {0: ("k", 1, 0, 0), 1: ("k", 1, 1, 0), 2: ("q", 1, 0, 0), 3: ("q", 1, 1, 0),
            4: ("y", 0, 0, -1), 5: ("o", 1, 1, -1), 6: ("y", 1, 0, -1), 7: ("y", 0, 1, -1), 8: ("y", 1, 1, -1),
            9: ("mean", 0, 0, 1), 10: ("v", 1, 0, 0), 11: ("var", 0, 0, 1), 12: ("v", 1, 1, 0), 13: ("o", 0, 0, 0),
            17: ("k", 0, 0, 1), 18: ("k", 0, 1, 1), 19: ("q", 0, 0, 1), 20: ("q", 0, 1, 1),
            21: ("v", 0, 0, 1), 22: ("v", 0, 1, 1), 23: ("o", 0, 1, 0), 29: ("o", 1, 0, 0)}
    FIRST_JOBS = [("k", 0, 0), ("q", 0, 0), ("k", 0, 1), ("q", 0, 1), ("v", 0, 0), ("v", 0, 1)]
    SPLIT = ("k", "q", "v", "o")

    ctx = ExitStack()
    with ctx:
        def sb(name, shape, dt=F32):
            return ctx.enter_context(nc.sbuf_tensor(name, shape, dt))

        def sem(name):
            return ctx.enter_context(nc.semaphore(name))

        ident = sb("ident", [P, P])
        ident16 = sb("ident16", [P, P], F16)
        group_avg = sb("group_avg", [P, P])
        w_in = {n: sb(f"w_in_{n}", [P, CT, C]) for n in "kqvp"}
        wT = {n: sb(f"wT_{n}", [P, CT, C]) for n in "kqvp"}
        w_sc = {n: sb(f"w_sc_{n}", [P, CT, C]) for n in "kqvp"}
        w_hi = {n: sb(f"w_hi_{n}", [P, CT, C], F16) for n in "kqvp"}
        w_lo = {n: sb(f"w_lo_{n}", [P, CT, C], F16) for n in "kqvp"}
        vec_rows = sb("vec_rows", [6 * CT, P])
        vec_cols = sb("vec_cols", [P, 6 * CT])
        vec = {n: vec_cols[:, CT * m:CT * (m + 1)] for m, n in enumerate(("gn_w", "gn_b", "k", "q", "v", "p"))}
        gam_sc = sb("gam_sc", [P, CT])
        w_gnb = sb("w_gnb", [P, 3, CT])
        bias = {n: sb(f"bias_{n}", [P, CT]) for n in "kqvp"}
        bias_s = {n: sb(f"bias_s_{n}", [P, CT]) for n in "kq"}
        wp_bv = sb("wp_bv", [P, CT])
        xin = sb("xin", [P, CT, HW])
        bn = sb("bn", [P, CT, 2, 6])
        mv = sb("mv", [P, CT, 2])
        gmean = sb("gmean", [P, CT])
        dev = sb("dev", [P, CT])
        dev2 = sb("dev2", [P, CT])
        gvar = sb("gvar", [P, CT])
        veps = sb("veps", [P, CT])
        expo = sb("expo", [P, CT])
        eps = sb("eps", [P, CT])
        rstd = sb("rstd", [P, CT])
        z_a = sb("z_a", [P, CT])
        z_hi = sb("z_hi", [P, CT, HW], F16)
        z_lo = sb("z_lo", [P, CT, HW], F16)
        e32 = {n: sb(f"e32_{n}", [P, 2, HALF]) for n in SPLIT}
        kq_hi = {n: sb(f"st_hi_{n}", [P, HW], F16) for n in "kq"}
        kq_lo = {n: sb(f"st_lo_{n}", [P, HW], F16) for n in "kq"}
        k_both = sb("k_both", [P, HEADS, HW], F16)
        q_twice = sb("q_twice", [P, HEADS, HW], F16)
        k_one = sb("k_one", [D + 1, HEADS, HW], F16)
        q_max = sb("q_max", [D + 1, HEADS, HW], F16)
        v_hi = sb("v_hi", [P, NK, HEADS, PV], F16)
        v_lo = sb("v_lo", [P, NK, HEADS, D], F16)
        mx8 = sb("mx8", [P, 2, QT, 2])
        mx4 = sb("mx4", [P, 2, QT])
        shift = sb("shift", [P, 2, QT], F16)
        shift_row = sb("shift_row", [QT, 2, P], F16)
        p32 = sb("p32", [P, SPU, CPS * HALF])
        p_hi = sb("p_hi", [P, PR, CPS, HALF], F16)
        p_lo = sb("p_lo", [P, PR, CPS, HALF], F16)
        rden = sb("rden", [P, 2, QT])
        o32 = sb("o32", [P, 2, QT, P])
        oT_hi = sb("oT_hi", [P, CT, HW], F16)
        oT_lo = sb("oT_lo", [P, CT, HW], F16)
        y32 = sb("y32", [P, CT, HW])
        xres = sb("xres", [P, CT, HW])

        def pb(name, n=1):
            return ctx.enter_context(nc.psum_tensor(name, [P, 512 * n], F32))

        st = [pb("st0", 2), pb("st1", 2)]
        mxb = [pb("mx0"), pb("mx1")]
        pv = pb("pv")
        gen = pb("gen")
        first_banks = [st[0][:, 0:512], st[0][:, 512:1024], st[1][:, 0:512], st[1][:, 512:1024], pv[:, :], gen]
        pv_v = pv[:, 0:QT * PV].rearrange("p (t n) -> p t n", n=PV)

        s_w = {n: sem(f"s_w_{n}") for n in "kqvp"}
        s_vec = sem("s_vec")
        s_xin = [sem(f"s_xin{t}") for t in range(CT)]
        s_xres = sem("s_xres")
        s_const = sem("s_const")
        s_cfill = sem("s_cfill")
        s_vecT = sem("s_vecT")
        s_cols = sem("s_cols")
        s_wT = sem("s_wT")
        s_gam = sem("s_gam")
        s_wraw = sem("s_wraw")
        s_wsc = sem("s_wsc")
        s_whi = sem("s_whi")
        s_wlo = sem("s_wlo")
        s_gnb = sem("s_gnb")
        s_bias = sem("s_bias")
        s_wpbv = sem("s_wpbv")
        s_mv = sem("s_mv")
        s_gmean = sem("s_gmean")
        s_dev = sem("s_dev")
        s_gvar = sem("s_gvar")
        s_za = sem("s_za")
        s_z32 = sem("s_z32")
        s_zhi = sem("s_zhi")
        s_zlo = sem("s_zlo")
        s_zlo_dve = sem("s_zlo_dve")
        s_gen_full = sem("s_gen_full")
        s_e32 = {n: sem(f"s_e32_{n}") for n in SPLIT}
        s_hi = {n: sem(f"s_hi_{n}") for n in SPLIT}
        s_lo = {n: sem(f"s_lo_{n}") for n in SPLIT}
        s_dup = {n: sem(f"s_dup_{n}") for n in "kq"}
        s_mx_full = sem("s_mx_full")
        s_mx_free = sem("s_mx_free")
        s_shift = sem("s_shift")
        s_shift_dma = sem("s_shift_dma")
        s_st = sem("s_st")
        s_exp = sem("s_exp")
        s_phi = sem("s_phi")
        s_plo_dve = sem("s_plo_dve")
        s_plo_pool = sem("s_plo_pool")
        s_pv = sem("s_pv")
        s_o32 = sem("s_o32")
        s_y = sem("s_y")
        s_yx = sem("s_yx")
        s_out = sem("s_out")
        s_ones = sem("s_ones")

        block = ctx.enter_context(nc.Block())

        def count(b, per, k):
            reg, n = b
            return per * n + k if reg is None else reg * per + (per * n + k)

        def before(b):
            return b[0], b[1] - 1

        def after(b):
            return b[0], b[1] + 1

        def wait(eng, s, b, per, k):
            v = count(b, per, k)
            assert b[0] is None or per * b[1] + k > 0
            if b[0] is not None or v > 0:
                eng.wait_ge(s, v)

        class Tally:

            def __init__(self, per):
                self.n, self.per, self.turn, self.start = 0, per, None, 0

            def add(self):
                self.n += 1

            def value(self):
                return self.n if self.turn is None else self.turn * self.per + self.n

            def enter(self, turn):
                self.turn, self.start = turn, self.n

            def leave(self):
                assert self.n - self.start == self.per
                self.turn = None
                self.n += self.per * (B - 2)

        class Latest:

            def __init__(self):
                self.job = None

            def enter(self, turn):
                self.job = (*self.job[:3], (turn, self.job[3][1]))

            def leave(self):
                self.job = (*self.job[:3], (None, self.job[3][1] + B - 2))

        def batches(eng, slot, tallies=()):
            for g in range(TURN):
                slot((None, 0), g, False, True, True)
            with eng.Fori(0, B - 1) as turn:
                for t in tallies:
                    t.enter(turn)
                for g in range(TURN, SLOTS):
                    slot((turn, 0), g, True, True, True)
                for g in range(TURN):
                    slot((turn, 1), g, True, True, True)
                for t in tallies:
                    t.leave()
            for g in range(TURN, SLOTS):
                slot((None, B - 1), g, True, False, True)
            for g in range(TURN):
                slot((None, B), g, True, False, False)

        def job_at(g, b, prev, nxt, cur):
            if g not in JOBS:
                return None
            kind, i, j, rel = JOBS[g]
            if not {-1: prev, 0: cur, 1: cur if kind == "mean" else nxt}[rel]:
                return None
            return kind, i, j, {-1: before(b), 0: b, 1: after(b)}[rel]

        def back(b, g, n, prev, cur):
            if g >= n:
                return (b, g - n) if cur else None
            return (before(b), g - n + SLOTS) if prev else None

        def ahead(b, g, slots, nxt, cur):
            u = (g + slots) // SPU
            if not cur:
                return None
            if u < UNITS:
                return b, u
            return (after(b), u - UNITS) if nxt else None

        def maxima_at(b, g, nxt, cur):
            return ahead(b, g, MX_AHEAD, nxt, cur), 2 * ((g + MX_AHEAD) % SPU)

        def shift_at(b, g, nxt, cur):
            return ahead(b, g, 2, nxt, cur) if g % SPU == 2 else None

        def unit(u):
            return 2 * (u // 4) + u % 2, (u // 2) % 2

        def lo_on_dve(g):
            return g % SPU in (1, 2)

        def wait_lo(eng, b, g):
            u, s = divmod(g, SPU)
            if lo_on_dve(g):
                wait(eng, s_plo_dve, b, 2 * UNITS, 2 * u + s)
            else:
                wait(eng, s_plo_pool, b, 2 * UNITS, 2 * u + (1 if s == 0 else 2))

        def v_parts(tile, i, j):
            return (tile[:, 4 * j:4 * j + 4, 2 * i:2 * i + 2, 0:D],
                    e32["v"][:, j, :].rearrange("p (c h d) -> p c h d", c=4, h=2))

        @block.sync
        def _(sp):
            sp.sem_inc(s_out, OUT_SEED)
            for t in range(CT):
                sp.dma_start(xin[:, t, :], x_v[0, :, t, :]).then_inc(s_xin[t], 16)
            for n, w in (("v", wv), ("p", wp)):
                sp.dma_start(w_in[n][:, :, :], w.rearrange("(t p) c -> p t c", p=P)).then_inc(s_w[n], 16)

            def image(b):
                return b[1] if b[0] is None else b[0] + b[1]

            def load_next(b, img):
                wait(sp, s_zlo, b, 1, 1)
                wait(sp, s_zlo_dve, b, 1, 1)
                for t in range(CT):
                    sp.dma_start(xin[:, t, :], x_v[img, :, t, :]).then_inc(s_xin[t], 16)

            def dup(n, p, b):
                wait(sp, s_lo[n], b, 4, 2 * p + 2)
                heads = slice(2 * p, 2 * p + 2)
                top, low = (k_both, k_one) if n == "k" else (q_twice, q_max)
                for dst, src in ((top[0:D, heads, :], kq_hi[n]),
                                 (top[D:P, heads, :], kq_lo[n] if n == "k" else kq_hi[n]),
                                 (low[0:D, heads, :], kq_hi[n] if n == "k" else kq_lo[n])):
                    for h in range(2):
                        sp.dma_start(dst[:, h, :], src[h * D:(h + 1) * D, :]).then_inc(s_dup[n], 16)

            def shift_to_row(b, u):
                head, half = unit(u)
                wait(sp, s_mx_free, b, MXJ * UNITS, MXJ * (u + 1))
                sp.dma_start(q_max[D:D + 1, head, half * HALF:(half + 1) * HALF],
                             shift_row[:, u % 2, :]).then_inc(s_shift_dma, 16)

            def slot(b, g, prev, nxt, cur):
                u, s = divmod(g, SPU)
                if g == 1 and prev:
                    sp.dma_start(xres[:, :, :], x_v[image(before(b))]).then_inc(s_xres, 16)
                if g == 3 and cur:
                    dup("k", 1, b)
                if g == 5 and cur:
                    dup("q", 1, b)
                if g == 9 and prev:
                    for j in range(4):
                        wait(sp, s_yx, before(b), 4, j + 1)
                        half = slice((j // 2) * HALF, (j // 2 + 1) * HALF)
                        sp.dma_start(out_v[image(before(b)), :, j % 2, half], y32[:, j % 2, half]).then_inc(s_out, 16)
                if g == 17 and nxt:
                    load_next(after(b), (b[0] + 2) % B)
                if g == 20 and nxt:
                    dup("k", 0, after(b))
                if g == 22 and nxt:
                    dup("q", 0, after(b))
                v = shift_at(b, g, nxt, cur)
                if v:
                    shift_to_row(*v)

            load_next((None, 0), 1)
            dup("k", 0, (None, 0))
            dup("q", 0, (None, 0))
            shift_to_row((None, 0), 0)
            batches(sp, slot)
            sp.wait_ge(s_out, 16 * 4 * B + OUT_SEED)

        @block.tensor
        def _(pe):
            latest = Latest()

            def bank_empty():
                if latest.job is None:
                    return
                kind, i, j, b = latest.job
                if kind in SPLIT:
                    wait(pe, s_e32[kind], b, 4, 2 * i + j + 1)
                elif kind == "y":
                    wait(pe, s_y, b, 4, i + 2 * j + 1)
                else:
                    wait(pe, {"mean": s_gmean, "var": s_gvar, "gnb": s_gnb, "wpbv": s_wpbv}[kind], b, 1, 1)

            def parts(dst, lhs, rhs, first=True):
                for t in range(CT):
                    (lh, ll), (rh, rl) = lhs(t), rhs(t)
                    for n, (a, c) in enumerate(((lh, rh), (lh, rl), (ll, rh))):
                        yield nc.tensor.matmul(dst, a, c, start=first and t == 0 and n == 0,
                                               stop=t == CT - 1 and n == 2, skip_group_check=True)

            def job(kind, i, j, b, bank=gen):
                if kind in "kqv":
                    wait(pe, s_zlo, b, 1, 1)
                    wait(pe, s_zlo_dve, b, 1, 1)
                if kind == "mean":
                    wait(pe, s_mv, b, 1, 1)
                if kind == "var":
                    wait(pe, s_dev, b, 1, 1)
                if kind == "o":
                    wait(pe, s_o32, b, UNITS, 4 * i + 2 * j + 2)
                if kind == "y":
                    wait(pe, s_lo["o"], b, 4, 3 + j)
                if bank is gen:
                    bank_empty()
                half = slice(j * HALF, (j + 1) * HALF)
                if kind in "kq":
                    o = slice(i * P, (i + 1) * P)
                    for mm in parts(bank[:, :], lambda t: (w_hi[kind][:, t, o], w_lo[kind][:, t, o]),
                                    lambda t: (z_hi[:, t, half], z_lo[:, t, half])):
                        last = mm
                if kind == "v":
                    o = slice(i * P, (i + 1) * P)
                    for c in range(4):
                        k = slice((4 * j + c) * P, (4 * j + c + 1) * P)
                        for mm in parts(bank[:, c * P:(c + 1) * P], lambda t: (z_hi[:, t, k], z_lo[:, t, k]),
                                        lambda t: (w_hi["v"][:, t, o], w_lo["v"][:, t, o]), first=c == 0):
                            last = mm
                if kind == "y":
                    o = slice(i * P, (i + 1) * P)
                    for mm in parts(bank[:, :], lambda t: (w_hi["p"][:, t, o], w_lo["p"][:, t, o]),
                                    lambda t: (oT_hi[:, t, half], oT_lo[:, t, half])):
                        last = mm
                if kind == "o":
                    for q in range(QT):
                        last = nc.tensor.transpose(bank[:, q * P:(q + 1) * P], o32[:, j, q, :], ident[:, :])
                if kind == "mean":
                    last = nc.tensor.matmul(bank[:, 0:CT], group_avg[:, :], mv[:, :, 0], start=True, stop=True)
                if kind == "var":
                    last = nc.tensor.matmul(bank[:, 0:CT], group_avg[:, :], dev2[:, :], start=True, stop=True)
                last.then_inc(s_gen_full, 1)
                if bank is gen:
                    latest.job = (kind, i, j, b)

            def maximum(b, u, j):
                head, half = unit(u)
                wait(pe, s_mx_free, b, MXJ * UNITS, MXJ * u + j - 1)
                q = half * HALF + (j // 2) * P
                nc.tensor.matmul(mxb[(MXJ * u + j) % 2][:, :], q_twice[:, head, q:q + P],
                                 k_both[:, head, (j % 2) * 512:(j % 2 + 1) * 512],
                                 start=True, stop=True).then_inc(s_mx_full, 1)

            def shift_transpose(b, u):
                j = MXJ - 1
                wait(pe, s_mx_free, b, MXJ * UNITS, MXJ * u + j - 1)
                wait(pe, s_shift, b, UNITS, u + 1)
                nc.tensor.matmul(mxb[(MXJ * u + j) % 2][0:QT, 0:P], shift[:, u % 2, :], ident16[:, :],
                                 start=True, stop=True).then_inc(s_mx_full, 1)

            def scores(b, g):
                u, s = divmod(g, SPU)
                head, half = unit(u)
                q = slice(half * HALF, (half + 1) * HALF)
                if s == 0:
                    wait(pe, s_shift_dma, b, 16 * UNITS, 16 * (u + 1))
                wait(pe, s_exp, b, SLOTS, g - 1)
                for c in range(CPS):
                    k = slice((CPS * s + c) * P, (CPS * s + c + 1) * P)
                    dst = st[g % 2][:, c * HALF:(c + 1) * HALF]
                    nc.tensor.matmul(dst, k_both[:, head, k], q_twice[:, head, q], start=True, stop=False)
                    last = nc.tensor.matmul(dst, k_one[:, head, k], q_max[:, head, q], start=False, stop=True)
                last.then_inc(s_st, 1)

            def weigh(b, g):
                u, s = divmod(g, SPU)
                head, _ = unit(u)
                wait(pe, s_phi, b, SLOTS, g + 1)
                wait_lo(pe, b, g)
                if s == 0:
                    wait(pe, s_o32, b, UNITS, u)
                    if u % 4 == 0:
                        wait(pe, s_lo["v"], b, 4, u // 2 + 2)
                for c in range(CPS):
                    k = CPS * s + c
                    for q in range(QT):
                        qs = slice(q * P, (q + 1) * P)
                        hi, lo = p_hi[:, g % PR, c, qs], p_lo[:, g % PR, c, qs]
                        nc.tensor.matmul(pv_v[:, q, :], hi, v_hi[:, k, head, :], start=k == 0 and q == 0,
                                         stop=False, skip_group_check=True)
                        nc.tensor.matmul(pv_v[:, q, 0:D], hi, v_lo[:, k, head, :], start=False, stop=False,
                                         skip_group_check=True)
                        last = nc.tensor.matmul(pv_v[:, q, :], lo, v_hi[:, k, head, :], start=False,
                                                stop=k == NK - 1, skip_group_check=True)
                last.then_inc(s_pv, 1)

            def slot(b, g, prev, nxt, cur):
                u, s = divmod(g, SPU)
                if cur:
                    scores(b, g)
                v = shift_at(b, g, nxt, cur)
                if v:
                    shift_transpose(*v)
                v, n = maxima_at(b, g, nxt, cur)
                if v:
                    if n == 0 and v[1] % 4 == 0:
                        for kind in "kq":
                            wait(pe, s_dup[kind], v[0], 16 * 12, 16 * 6 * (v[1] // 4 + 1))
                    maximum(*v, n)
                todo = job_at(g, b, prev, nxt, cur)
                if todo:
                    job(*todo)
                if v:
                    maximum(*v, n + 1)
                old = back(b, g, LAG, prev, cur)
                if old:
                    weigh(*old)

            pe.wait_ge(s_const, 3)
            pe.wait_ge(s_vec, 16 * 6)
            nc.tensor.transpose(pv[:, 0:6 * CT], vec_rows[:, :], ident[0:6 * CT, 0:6 * CT]).then_inc(s_vecT, 1)
            for m, n in enumerate("kqvp"):
                pe.wait_ge(s_w[n], 16)
                for t in range(CT):
                    for o in range(CT):
                        last = nc.tensor.transpose(st[m // 2][:, (m % 2) * 512 + t * C + o * P:][:, 0:P],
                                                   w_in[n][:, o, t * P:(t + 1) * P], ident[:, :])
                last.then_inc(s_wT, 1)
            job("mean", 0, 0, (None, 0))
            job("var", 0, 0, (None, 0))
            pe.wait_ge(s_wraw, 3)
            pe.wait_ge(s_cols, 1)
            bank_empty()
            for m, n in enumerate("kqv"):
                for o in range(CT):
                    for t in range(CT):
                        last = nc.tensor.matmul(gen[:, m * CT + o:m * CT + o + 1], wT[n][:, t, o * P:(o + 1) * P],
                                                vec["gn_b"][:, t:t + 1], start=m == o == t == 0, stop=t == CT - 1,
                                                skip_group_check=True)
            last.then_inc(s_gen_full, 1)
            latest.job = ("gnb", 0, 0, (None, 0))
            pe.wait_ge(s_wlo, 3)
            pe.wait_ge(s_wsc, 4 * CT)
            for (kind, i, j), bank in zip(FIRST_JOBS, first_banks):
                job(kind, i, j, (None, 0), bank)
            for n in "kq":
                pe.wait_ge(s_dup[n], 16 * 6)
            pe.wait_ge(s_ones, 2)
            for j in range(MXJ - 1):
                maximum((None, 0), 0, j)
            pe.wait_ge(s_bias, 3)
            pe.wait_ge(s_wlo, 4)
            bank_empty()
            for o in range(CT):
                for t in range(CT):
                    last = nc.tensor.matmul(gen[:, o:o + 1], wT["p"][:, t, o * P:(o + 1) * P],
                                            bias["v"][:, t:t + 1], start=o == t == 0, stop=t == CT - 1,
                                            skip_group_check=True)
            last.then_inc(s_gen_full, 1)
            latest.job = ("wpbv", 0, 0, (None, 0))
            shift_transpose((None, 0), 0)
            for j in range(4):
                maximum((None, 0), 1, j)
            for kind, n in (("k", 2), ("q", 2), ("v", 2)):
                pe.wait_ge(s_e32[kind], n)
            batches(pe, slot, [latest])

        @block.scalar
        def _(act):
            jobs = Tally(len(JOBS))

            act.dma_start(w_in["k"][:, :, :], wk.rearrange("(t p) c -> p t c", p=P)).then_inc(s_w["k"], 16)
            act.dma_start(w_in["q"][:, :, :], wq.rearrange("(t p) c -> p t c", p=P)).then_inc(s_w["q"], 16)
            for m, a in enumerate((gn_w, gn_b, bk, bq, bv, bp)):
                act.dma_start(vec_rows[CT * m:CT * (m + 1), :], a.rearrange("(t p) -> t p", p=P)).then_inc(s_vec, 16)

            def job(kind, i, j, b, bank=gen):
                jobs.add()
                act.wait_ge(s_gen_full, jobs.value())
                if kind in SPLIT and not (kind == "o" and i == 0):
                    wait(act, s_lo[kind], b, 4, max(2 * i + j - 1, 0))
                if kind in "kq":
                    last = nc.scalar.activation(e32[kind][:, j, :], bank[:, :], ACT.Identity,
                                                bias=bias_s[kind][:, i:i + 1],
                                                scale=QKV_SCALE / (Z_SCALE * W_SCALE))
                if kind == "v":
                    last = nc.scalar.activation(e32[kind][:, j, :], bank[:, :], ACT.Copy,
                                                scale=QKV_SCALE / (Z_SCALE * W_SCALE))
                if kind == "o":
                    last = nc.scalar.activation(e32[kind][:, j, :], bank[:, :], ACT.Copy, scale=O_SCALE)
                if kind in SPLIT:
                    last.then_inc(s_e32[kind], 1)
                if kind == "y":
                    act.wait_ge(s_bias, 4)
                    wait(act, s_out, b, 64, OUT_SEED)
                    last = nc.scalar.activation(y32[:, i, j * HALF:(j + 1) * HALF], bank[:, :], ACT.Identity,
                                                bias=bias["p"][:, i:i + 1], scale=1.0 / (O_SCALE * W_SCALE))
                    last.then_inc(s_y, 1)
                if kind == "mean":
                    nc.scalar.activation(gmean[:, :], bank[:, 0:CT], ACT.Copy).then_inc(s_gmean, 1)
                if kind == "var":
                    nc.scalar.activation(gvar[:, :], bank[:, 0:CT], ACT.Copy).then_inc(s_gvar, 1)

            def slot(b, g, prev, nxt, cur):
                u, s = divmod(g, SPU)
                if cur:
                    wait(act, s_st, b, SLOTS, g + 1)
                    if g >= SPU or prev:
                        wait_lo(act, *back(b, g, SPU, prev, cur))
                    nc.scalar.activation(p32[:, s, :], st[g % 2][:, :], ACT.Exp, scale=SM_SCALE / M_SCALE)\
                      .then_inc(s_exp, 1)
                    wait(act, s_exp, b, SLOTS, g + 1)
                    wait(act, s_pv, b, SLOTS, g + 1 - PR)
                    nc.scalar.activation(p_hi[:, g % PR, :, :], p32[:, s, :].rearrange("p (c n) -> p c n", n=HALF),
                                         ACT.Copy).then_inc(s_phi, 1)
                todo = job_at(g, b, prev, nxt, cur)
                if todo:
                    job(*todo)
                if g in (14, 15) and nxt:
                    z_high(after(b), g - 14)

            def z_high(b, t):
                wait(act, s_z32, b, CT, t + 1)
                nc.scalar.activation(z_hi[:, t, :], xin[:, t, :], ACT.Copy).then_inc(s_zhi, 1)

            def from_bank(dst, signal):
                jobs.add()
                act.wait_ge(s_gen_full, jobs.value())
                nc.scalar.activation(dst, gen[:, 0:dst.free_size()], ACT.Copy).then_inc(signal, 1)

            def split_weights(m, n):
                act.wait_ge(s_wT, m + 1)
                src = st[m // 2][:, (m % 2) * 512:(m % 2 + 1) * 512].rearrange("p (t o) -> p t o", t=CT)
                nc.scalar.activation(wT[n][:, :, :], src, ACT.Copy).then_inc(s_wraw, 1)
                for t in range(CT):
                    scale = W_SCALE if n == "p" else gam_sc[:, t:t + 1]
                    nc.scalar.activation(w_sc[n][:, t, :], src[:, t, :], ACT.Copy, scale=scale).then_inc(s_wsc, 1)
                act.wait_ge(s_wsc, CT * (m + 1))
                nc.scalar.activation(w_hi[n][:, :, :], w_sc[n][:, :, :], ACT.Copy).then_inc(s_whi, 1)

            act.wait_ge(s_gam, 1)
            split_weights(0, "k")
            split_weights(1, "q")
            job("mean", 0, 0, (None, 0))
            split_weights(2, "v")
            job("var", 0, 0, (None, 0))
            split_weights(3, "p")
            from_bank(w_gnb[:, :, :].rearrange("p n o -> p (n o)"), s_gnb)
            z_high((None, 0), 0)
            z_high((None, 0), 1)
            act.wait_ge(s_bias, 2)
            for (kind, i, j), bank in zip(FIRST_JOBS, first_banks):
                job(kind, i, j, (None, 0), bank)
            from_bank(wp_bv[:, :], s_wpbv)
            batches(act, slot, [jobs])

        @block.vector
        def _(dve):
            def then(ins):
                dve.drain()

            def row_max(b, u, j):
                wait(dve, s_mx_full, b, MXJ * UNITS, MXJ * u + j + 1)
                nc.vector.reduce_max(mx8[:, u % 2, j // 2, j % 2:j % 2 + 1], mxb[(MXJ * u + j) % 2][:, :], AX.X)\
                  .then_inc(s_mx_free, 1)

            def make_shift(b, u):
                wait(dve, s_mx_free, b, MXJ * UNITS, MXJ * u + 2 * QT)
                then(nc.vector.reduce_max(mx4[:, u % 2, :], mx8[:, u % 2, :, :], AX.X))
                nc.vector.tensor_scalar(shift[:, u % 2, :], mx4[:, u % 2, :], -1.0 / M_SCALE, P_LOG / SM_SCALE,
                                        ALU.mult, ALU.add).then_inc(s_shift, 1)

            def row_out(b, u):
                wait(dve, s_mx_full, b, MXJ * UNITS, MXJ * (u + 1))
                wait(dve, s_shift_dma, b, 16 * UNITS, 16 * (u - 1))
                nc.vector.tensor_copy(shift_row[:, u % 2, :], mxb[(MXJ * u + MXJ - 1) % 2][0:QT, 0:P])\
                  .then_inc(s_mx_free, 1)

            def high(kind, i, j, b):
                wait(dve, s_e32[kind], b, 4, 2 * i + j + 1)
                half = slice(j * HALF, (j + 1) * HALF)
                src = e32[kind][:, j, :]
                if kind in "kq":
                    wait(dve, s_dup[kind], b, 16 * 12, 16 * 6 * i)
                    dst = kq_hi[kind][:, half]
                if kind == "v":
                    dst, src = v_parts(v_hi, i, j)
                if kind == "o":
                    dst = oT_hi[:, i, half]
                nc.vector.tensor_copy(dst, src).then_inc(s_hi[kind], 1)

            def normalise(b, u):
                head, half = unit(u)
                wait(dve, s_pv, b, SLOTS, SPU * (u + 1))
                then(nc.vector.reciprocal(rden[:, u % 2, :], pv_v[:, :, D]))
                nc.vector.tensor_tensor(o32[:, half, :, (u % 2) * D:(u % 2 + 1) * D], pv_v[:, :, 0:D],
                                        rden[:, u % 2, :].unsqueeze(2).to_broadcast([P, QT, D]), ALU.mult)\
                  .then_inc(s_o32, 1)

            def channel_stats(b, t):
                wait(dve, s_xin[t], b, 16, 16)
                for n in range(2):
                    then(nc.vector.bn_stats(bn[:, t, n, :], xin[:, t, n * 512:(n + 1) * 512]))
                ins = nc.vector.bn_aggr(mv[:, t, :], bn[:, t, :, :].rearrange("p n s -> p (n s)"))
                if t == CT - 1:
                    ins.then_inc(s_mv, 1)

            def about_group_mean(b):
                wait(dve, s_gmean, b, 1, 1)
                wait(dve, s_mv, b, 1, 1)
                then(nc.vector.tensor_tensor(dev[:, :], mv[:, :, 0], gmean[:, :], ALU.subtract))
                then(nc.vector.tensor_tensor(dev[:, :], dev[:, :], dev[:, :], ALU.mult))
                nc.vector.tensor_tensor(dev2[:, :], dev[:, :], mv[:, :, 1], ALU.add).then_inc(s_dev, 1)

            def z_of(b, t):
                wait(dve, s_za, b, 1, 1)
                nc.vector.tensor_scalar(xin[:, t, :], xin[:, t, :], gmean[:, t:t + 1], z_a[:, t:t + 1],
                                        ALU.subtract, ALU.mult).then_inc(s_z32, 1)

            def z_low_dve(b):
                wait(dve, s_zhi, b, CT, CT)
                nc.vector.tensor_tensor(z_lo[:, CT - 1, :], xin[:, CT - 1, :], z_hi[:, CT - 1, :], ALU.subtract)\
                  .then_inc(s_zlo_dve, 1)

            def slot(b, g, prev, nxt, cur):
                old = back(b, g, LAG + 1, prev, cur)
                if old and old[1] % SPU == SPU - 1:
                    normalise(old[0], old[1] // SPU)
                v = shift_at(b, g, nxt, cur)
                if v:
                    row_out(*v)
                v, n = maxima_at(b, g, nxt, cur)
                if v:
                    row_max(*v, n)
                todo = job_at(g - 1, b, prev, nxt, cur)
                if todo and todo[0] in SPLIT:
                    high(*todo)
                old = back(b, g, 1, prev, cur)
                if old and lo_on_dve(old[1]):
                    wait(dve, s_phi, old[0], SLOTS, old[1] + 1)
                    nc.vector.tensor_tensor(p_lo[:, old[1] % PR, :, :],
                                            p32[:, old[1] % SPU, :].rearrange("p (c n) -> p c n", n=HALF),
                                            p_hi[:, old[1] % PR, :, :], ALU.subtract).then_inc(s_plo_dve, 1)
                if v:
                    row_max(*v, n + 1)
                    if n == 2 * QT - 2:
                        make_shift(*v)
                if g in (1, 5) and cur:
                    channel_stats(after(b), g // 4)
                if g == TURN and nxt:
                    about_group_mean(after(b))
                if g == 13 and nxt:
                    for t in range(CT):
                        z_of(after(b), t)
                if g == 16 and nxt:
                    z_low_dve(after(b))

            nc.vector.memset(v_hi[:, :, :, D], QKV_SCALE).then_inc(s_ones, 1)
            dve.wait_ge(s_vecT, 1)
            nc.vector.tensor_copy(vec_cols[:, :], pv[:, 0:6 * CT]).then_inc(s_cols, 1)
            dve.wait_ge(s_cols, 1)
            nc.vector.tensor_scalar(gam_sc[:, :], vec["gn_w"], W_SCALE, None, ALU.mult).then_inc(s_gam, 1)
            for t in range(CT):
                channel_stats((None, 0), t)
            about_group_mean((None, 0))
            for t in range(CT):
                z_of((None, 0), t)
            dve.wait_ge(s_gnb, 1)
            for m, n in enumerate("kqv"):
                ins = nc.vector.tensor_tensor(bias[n][:, :], w_gnb[:, m, :], vec[n], ALU.add)
                if n == "v":
                    ins.then_inc(s_bias, 1)
                else:
                    then(ins)
                    nc.vector.tensor_scalar(bias_s[n][:, :], bias[n][:, :], QKV_SCALE, None, ALU.mult)\
                      .then_inc(s_bias, 1)
            z_low_dve((None, 0))
            for kind, i, j in FIRST_JOBS[:4]:
                high(kind, i, j, (None, 0))
                if kind == "q":
                    dve.wait_ge(s_hi["q"], j + 1)
                    half = slice(j * HALF, (j + 1) * HALF)
                    nc.vector.tensor_tensor(kq_lo["q"][:, half], e32["q"][:, j, :], kq_hi["q"][:, half],
                                            ALU.subtract).then_inc(s_lo["q"], 1)
            for kind, i, j in FIRST_JOBS[4:]:
                high(kind, i, j, (None, 0))
            for j in range(MXJ - 1):
                row_max((None, 0), 0, j)
            make_shift((None, 0), 0)
            row_out((None, 0), 0)
            for j in range(4):
                row_max((None, 0), 1, j)
            dve.wait_ge(s_wpbv, 1)
            nc.vector.tensor_tensor(bias["p"][:, :], wp_bv[:, :], vec["p"], ALU.add).then_inc(s_bias, 1)
            batches(dve, slot)

        @block.gpsimd
        def _(pool):
            def then(ins):
                pool.drain()

            def low(kind, i, j, b):
                wait(pool, s_hi[kind], b, 4, 2 * i + j + 1)
                half = slice(j * HALF, (j + 1) * HALF)
                src = e32[kind][:, j, :]
                if kind in "kq":
                    hi, lo = kq_hi[kind][:, half], kq_lo[kind][:, half]
                if kind == "v":
                    (hi, src), (lo, _) = v_parts(v_hi, i, j), v_parts(v_lo, i, j)
                if kind == "o":
                    hi, lo = oT_hi[:, i, half], oT_lo[:, i, half]
                nc.gpsimd.tensor_tensor(lo, src, hi, ALU.subtract).then_inc(s_lo[kind], 1)

            def residual(i, half, b):
                j = i + 2 * half
                wait(pool, s_y, b, 4, j + 1)
                wait(pool, s_xres, b, 16, 16)
                n = slice(half * HALF, (half + 1) * HALF)
                nc.gpsimd.tensor_tensor(y32[:, i, n], y32[:, i, n], xres[:, i, n], ALU.add).then_inc(s_yx, 1)

            def norm_factors(b):
                wait(pool, s_gvar, b, 1, 1)
                then(nc.gpsimd.tensor_tensor(veps[:, :], gvar[:, :], eps[:, :], ALU.add))
                then(nc.gpsimd.tensor_tensor(rstd[:, :], veps[:, :], expo[:, :], ALU.pow))
                then(nc.gpsimd.tensor_tensor(z_a[:, :], rstd[:, :], rstd[:, :], ALU.mult))
                then(nc.gpsimd.tensor_tensor(z_a[:, :], z_a[:, :], veps[:, :], ALU.mult))
                then(nc.gpsimd.tensor_scalar(z_a[:, :], z_a[:, :], -0.5 * Z_SCALE, 1.5 * Z_SCALE, ALU.mult, ALU.add))
                nc.gpsimd.tensor_tensor(z_a[:, :], z_a[:, :], rstd[:, :], ALU.mult).then_inc(s_za, 1)

            def z_low(b):
                wait(pool, s_zhi, b, CT, 1)
                nc.gpsimd.tensor_tensor(z_lo[:, 0, :], xin[:, 0, :], z_hi[:, 0, :], ALU.subtract).then_inc(s_zlo, 1)

            def slot(b, g, prev, nxt, cur):
                todo = job_at(g - 1, b, prev, nxt, cur)
                if todo and todo[0] in SPLIT:
                    low(*todo)
                old = back(b, g, 1, prev, cur)
                if old and not lo_on_dve(old[1]):
                    wait(pool, s_phi, old[0], SLOTS, old[1] + 1)
                    nc.gpsimd.tensor_tensor(p_lo[:, old[1] % PR, :, :],
                                            p32[:, old[1] % SPU, :].rearrange("p (c n) -> p c n", n=HALF),
                                            p_hi[:, old[1] % PR, :, :], ALU.subtract).then_inc(s_plo_pool, 1)
                if todo and todo[0] == "y":
                    residual(*todo[1:])
                if g == 12 and nxt:
                    norm_factors(after(b))
                if g == 15 and nxt:
                    z_low(after(b))

            nc.gpsimd.memset(ident[:, :], 0.0).then_inc(s_cfill, 1)
            nc.gpsimd.memset(ident16[:, :], 0.0).then_inc(s_cfill, 1)
            nc.gpsimd.memset(group_avg[:, :], 1.0 / GROUP).then_inc(s_cfill, 1)
            nc.gpsimd.memset(expo[:, :], -0.5).then_inc(s_cfill, 1)
            nc.gpsimd.memset(eps[:, :], EPS).then_inc(s_cfill, 1)
            pool.wait_ge(s_cfill, 5)
            for m in (ident, ident16):
                nc.gpsimd.affine_select(out=m[:, :], in_=m[:, :], compare_op=ALU.not_equal, fill=1.0, base=0,
                                        pattern=[[-1, P]], channel_multiplier=1).then_inc(s_const, 1)
            blocks = group_avg[:, :].rearrange("p (g n) -> p g n", n=GROUP)
            then(nc.gpsimd.affine_select(out=blocks, in_=blocks, compare_op=ALU.is_ge, fill=0.0, base=0,
                                         pattern=[[-GROUP, P // GROUP], [0, GROUP]], channel_multiplier=1))
            nc.gpsimd.affine_select(out=blocks, in_=blocks, compare_op=ALU.is_ge, fill=0.0, base=GROUP - 1,
                                    pattern=[[GROUP, P // GROUP], [0, GROUP]], channel_multiplier=-1)\
              .then_inc(s_const, 1)
            pool.drain()
            nc.gpsimd.memset(k_one[D:D + 1, :, :], M_SCALE).then_inc(s_ones, 1)
            pool.drain()
            for m, n in enumerate("kqvp"):
                pool.wait_ge(s_whi, m + 1)
                nc.gpsimd.tensor_tensor(w_lo[n][:, :, :], w_sc[n][:, :, :], w_hi[n][:, :, :], ALU.subtract)\
                  .then_inc(s_wlo, 1)
            norm_factors((None, 0))
            z_low((None, 0))
            for kind, i, j in FIRST_JOBS:
                if kind != "q":
                    low(kind, i, j, (None, 0))
            batches(pool, slot)


_INS = ["x", "L0_conv_gn_w", "L0_conv_gn_b", "L0_conv_wq", "L0_conv_bq", "L0_conv_wk", "L0_conv_bk",
        "L0_conv_wv", "L0_conv_bv", "L0_conv_wp", "L0_conv_bp"]


def kernel(**inputs):
    import numpy as _np
    import concourse.bacc as _bacc
    from concourse import mybir as _mybir
    from concourse.bass_utils import run_bass_kernel_spmd as _run

    nc = _bacc.Bacc("TRN2", target_bir_lowering=False, num_devices=1)
    arrays, args = {}, []
    for name in _INS:
        a = _np.ascontiguousarray(inputs[name])
        arrays[f"in_{name}_dram"] = a
        args.append(nc.dram_tensor(f"in_{name}_dram", a.shape, _mybir.dt.from_np(a.dtype), kind="ExternalInput").ap())
    shape = inputs["x"].shape
    args.append(nc.dram_tensor("out_0_dram", shape, _mybir.dt.float32, kind="ExternalOutput").ap())
    attention_block(nc, *args)
    r = _run(nc, [arrays], core_ids=[0])
    return r.results[0]["out_0_dram"]
```

```python
from contextlib import ExitStack

import concourse.bass as bass
from concourse import mybir

F32 = mybir.dt.float32
F16 = mybir.dt.float16
ALU = mybir.AluOpType
ACT = mybir.ActivationFunctionType
AX = mybir.AxisListType


def attention_block(nc, x, gn_w, gn_b, wq, bq, wk, bk, wv, bv, wp, bp, out):
    B, C, IH, IW = x.shape
    HW = IH * IW
    P = 128
    HEADS = 4
    D = C // HEADS
    GROUP = C // 32
    CT = C // P
    NK = HW // P
    HALF = HW // 2
    QT = HALF // P
    UNITS = HEADS * 2
    SPU = 4
    CPS = NK // SPU
    SLOTS = UNITS * SPU
    LAG = 4
    TURN = 13
    MX_AHEAD = 6
    MXJ = 2 * QT + 1
    PR = 8
    PV = D + 1
    EPS = 1e-5
    OUT_SEED = 16

    Z_SCALE = 512.0
    W_SCALE = 1024.0
    QKV_SCALE = 32.0
    M_SCALE = QKV_SCALE * QKV_SCALE
    O_SCALE = 128.0
    P_LOG = 8.317766166719343
    SM_SCALE = D ** -0.5

    x_v = x.rearrange("b (t p) h w -> b p t (h w)", p=P)
    out_v = out.rearrange("b (t p) h w -> b p t (h w)", p=P)

    JOBS = {0: ("k", 1, 1, 0), 1: ("y", 0, 0, -1), 2: ("q", 1, 1, 0), 3: ("v", 1, 0, 0), 4: ("mean", 0, 0, 1),
            5: ("o", 1, 1, -1), 6: ("var", 0, 0, 1), 8: ("y", 1, 0, -1), 9: ("y", 0, 1, -1), 10: ("y", 1, 1, -1),
            11: ("v", 1, 1, 0), 13: ("o", 0, 0, 0), 15: ("k", 0, 0, 1), 16: ("k", 0, 1, 1), 18: ("q", 0, 0, 1),
            20: ("q", 0, 1, 1), 22: ("v", 0, 0, 1), 23: ("o", 0, 1, 0), 24: ("v", 0, 1, 1), 26: ("k", 1, 0, 1),
            28: ("q", 1, 0, 1), 29: ("o", 1, 0, 0)}
    TAIL_JOBS = {0: ("y", 0, 0, -1), 3: ("y", 1, 0, -1), 5: ("o", 1, 1, -1), 8: ("y", 0, 1, -1), 10: ("y", 1, 1, -1)}
    FIRST_JOBS = [("k", 0, 0), ("k", 0, 1), ("q", 0, 0), ("q", 0, 1), ("k", 1, 0), ("q", 1, 0),
                  ("v", 0, 0), ("v", 0, 1)]
    LONG = ("k", "q", "v", "y")
    SPLIT = ("k", "q", "v", "o")

    ctx = ExitStack()
    with ctx:
        def sb(name, shape, dt=F32):
            return ctx.enter_context(nc.sbuf_tensor(name, shape, dt))

        def sem(name):
            return ctx.enter_context(nc.semaphore(name))

        ident = sb("ident", [P, P])
        ident16 = sb("ident16", [P, P], F16)
        group_avg = sb("group_avg", [P, P])
        w_in = {n: sb(f"w_in_{n}", [P, CT, C]) for n in "kqvp"}
        wT = {n: sb(f"wT_{n}", [P, CT, C]) for n in "kqvp"}
        w_sc = {n: sb(f"w_sc_{n}", [P, CT, C]) for n in "kqvp"}
        w_hi = {n: sb(f"w_hi_{n}", [P, CT, C], F16) for n in "kqvp"}
        w_lo = {n: sb(f"w_lo_{n}", [P, CT, C], F16) for n in "kqvp"}
        vec_rows = sb("vec_rows", [6 * CT, P])
        vec_cols = sb("vec_cols", [P, 6 * CT])
        vec = {n: vec_cols[:, CT * m:CT * (m + 1)] for m, n in enumerate(("gn_w", "gn_b", "k", "q", "v", "p"))}
        gam_sc = sb("gam_sc", [P, CT])
        w_gnb = sb("w_gnb", [P, 3, CT])
        bias = {n: sb(f"bias_{n}", [P, CT]) for n in "kqvp"}
        bias_s = {n: sb(f"bias_s_{n}", [P, CT]) for n in "kq"}
        wp_bv = sb("wp_bv", [P, CT])
        xin = sb("xin", [P, CT, HW])
        bn = sb("bn", [P, CT, 2, 6])
        mv = sb("mv", [P, CT, 2])
        gmean = sb("gmean", [P, CT])
        dev = sb("dev", [P, CT])
        dev2 = sb("dev2", [P, CT])
        gvar = sb("gvar", [P, CT])
        veps = sb("veps", [P, CT])
        expo = sb("expo", [P, CT])
        eps = sb("eps", [P, CT])
        first_use = sb("first_use", [P, CT])
        rstd = sb("rstd", [P, CT])
        z_a = sb("z_a", [P, CT])
        z_hi = sb("z_hi", [P, CT, HW], F16)
        z_lo = sb("z_lo", [P, CT, HW], F16)
        e32 = {n: sb(f"e32_{n}", [P, 2, HALF]) for n in SPLIT}
        kq_hi = {n: sb(f"st_hi_{n}", [P, HW], F16) for n in "kq"}
        kq_lo = {n: sb(f"st_lo_{n}", [P, HW], F16) for n in "kq"}
        k_both = sb("k_both", [P, HEADS, HW], F16)
        q_twice = sb("q_twice", [P, HEADS, HW], F16)
        k_one = sb("k_one", [D + 1, HEADS, HW], F16)
        q_max = sb("q_max", [D + 1, HEADS, HW], F16)
        v_hi = sb("v_hi", [P, NK, HEADS, PV], F16)
        v_lo = sb("v_lo", [P, NK, HEADS, D], F16)
        mx8 = sb("mx8", [P, 2, QT, 2])
        mx4 = sb("mx4", [P, 2, QT])
        shift = sb("shift", [P, 2, QT], F16)
        shift_row = sb("shift_row", [QT, 2, P], F16)
        p32 = sb("p32", [P, SPU, CPS * HALF])
        p_hi = sb("p_hi", [P, PR, CPS, HALF], F16)
        p_lo = sb("p_lo", [P, PR, CPS, HALF], F16)
        rden = sb("rden", [P, 2, QT])
        o32 = sb("o32", [P, 2, QT, P])
        oT_hi = sb("oT_hi", [P, CT, HW], F16)
        oT_lo = sb("oT_lo", [P, CT, HW], F16)
        y32 = sb("y32", [P, CT, HW])
        xres = sb("xres", [P, CT, HW])

        def pb(name, n=1):
            return ctx.enter_context(nc.psum_tensor(name, [P, 512 * n], F32))

        st = [pb("st0", 2), pb("st1", 2)]
        mxb = [pb("mx0"), pb("mx1")]
        pv = pb("pv")
        gen = pb("gen")
        weight_banks = [st[0][:, 0:512], st[0][:, 512:1024], st[1][:, 0:512], mxb[0]]
        first_banks = [st[0][:, 0:512], st[0][:, 512:1024], st[1][:, 0:512], st[1][:, 512:1024],
                       st[0][:, 0:512], st[0][:, 512:1024], st[1][:, 0:512], st[1][:, 512:1024]]
        pv_v = pv[:, 0:QT * PV].rearrange("p (t n) -> p t n", n=PV)

        s_w = {n: sem(f"s_w_{n}") for n in "kqvp"}
        s_vec = sem("s_vec")
        s_xin = [sem(f"s_xin{t}") for t in range(CT)]
        s_xres = sem("s_xres")
        s_const = sem("s_const")
        s_cfill = sem("s_cfill")
        s_vecT = sem("s_vecT")
        s_cols = sem("s_cols")
        s_wT = sem("s_wT")
        s_gam = sem("s_gam")
        s_wraw = sem("s_wraw")
        s_wsc = sem("s_wsc")
        s_whi = sem("s_whi")
        s_wlo = sem("s_wlo")
        s_gnb = sem("s_gnb")
        s_gnb_v = sem("s_gnb_v")
        s_bias = sem("s_bias")
        s_wpbv = sem("s_wpbv")
        s_mv = sem("s_mv")
        s_gmean = sem("s_gmean")
        s_dev = sem("s_dev")
        s_gvar = sem("s_gvar")
        s_za = sem("s_za")
        s_z32 = sem("s_z32")
        s_zhi = sem("s_zhi")
        s_zlo = sem("s_zlo")
        s_zlo_dve = sem("s_zlo_dve")
        s_gen_full = sem("s_gen_full")
        s_e32 = {n: sem(f"s_e32_{n}") for n in SPLIT}
        s_hi = {n: sem(f"s_hi_{n}") for n in SPLIT}
        s_lo = {n: sem(f"s_lo_{n}") for n in SPLIT}
        s_dup = {n: sem(f"s_dup_{n}") for n in "kq"}
        s_first = {n: [sem(f"s_first_{n}{h}") for h in range(2)] for n in "kq"}
        s_first_low = {n: sem(f"s_first_low_{n}") for n in "kq"}
        s_mx_full = sem("s_mx_full")
        s_mx_free = sem("s_mx_free")
        s_shift = sem("s_shift")
        s_shift_dma = sem("s_shift_dma")
        s_st = sem("s_st")
        s_exp = sem("s_exp")
        s_phi = sem("s_phi")
        s_plo_dve = sem("s_plo_dve")
        s_plo_pool = sem("s_plo_pool")
        s_pv = sem("s_pv")
        s_o32 = sem("s_o32")
        s_y = sem("s_y")
        s_yx = sem("s_yx")
        s_out = sem("s_out")
        s_ones = sem("s_ones")

        block = ctx.enter_context(nc.Block())

        def count(b, per, k):
            reg, n = b
            return per * n + k if reg is None else reg * per + (per * n + k)

        def before(b):
            return b[0], b[1] - 1

        def after(b):
            return b[0], b[1] + 1

        def wait(eng, s, b, per, k):
            v = count(b, per, k)
            assert b[0] is None or per * b[1] + k > 0
            if b[0] is not None or v > 0:
                eng.wait_ge(s, v)

        class Tally:

            def __init__(self, per):
                self.n, self.per, self.turn, self.start = 0, per, None, 0

            def add(self):
                self.n += 1

            def value(self):
                return self.n if self.turn is None else self.turn * self.per + self.n

            def enter(self, turn):
                self.turn, self.start = turn, self.n

            def leave(self):
                assert self.n - self.start == self.per
                self.turn = None
                self.n += self.per * (B - 2)

        class Latest:

            def __init__(self):
                self.job = None

            def enter(self, turn):
                self.job = (*self.job[:3], (turn, self.job[3][1]))

            def leave(self):
                self.job = (*self.job[:3], (None, self.job[3][1] + B - 2))

        def batches(eng, slot, tallies=()):
            for g in range(TURN):
                slot((None, 0), g, False, True, True)
            with eng.Fori(0, B - 1) as turn:
                for t in tallies:
                    t.enter(turn)
                for g in range(TURN, SLOTS):
                    slot((turn, 0), g, True, True, True)
                for g in range(TURN):
                    slot((turn, 1), g, True, True, True)
                for t in tallies:
                    t.leave()
            for g in range(TURN, SLOTS):
                slot((None, B - 1), g, True, False, True)
            for g in range(TURN):
                slot((None, B), g, True, False, False)

        def job_at(g, b, prev, nxt, cur):
            table = JOBS if cur else TAIL_JOBS
            if g not in table:
                return None
            kind, i, j, rel = table[g]
            if not {-1: prev, 0: cur, 1: cur if kind in ("mean", "var") else nxt}[rel]:
                return None
            return kind, i, j, {-1: before(b), 0: b, 1: after(b)}[rel]

        def tail_bank(g, cur):
            return st[0][:, 0:512] if not cur and g == max(TAIL_JOBS) else gen

        def back(b, g, n, prev, cur):
            if g >= n:
                return (b, g - n) if cur else None
            return (before(b), g - n + SLOTS) if prev else None

        def ahead(b, g, slots, nxt, cur):
            u = (g + slots) // SPU
            if not cur:
                return None
            if u < UNITS:
                return b, u
            return (after(b), u - UNITS) if nxt else None

        def maxima_at(b, g, nxt, cur):
            return ahead(b, g, MX_AHEAD, nxt, cur), 2 * ((g + MX_AHEAD) % SPU)

        def shift_at(b, g, nxt, cur):
            return ahead(b, g, 2, nxt, cur) if g % SPU == 2 else None

        def long_at(g, b, prev, nxt, cur):
            todo = job_at(g, b, prev, nxt, cur)
            return todo is not None and todo[0] in LONG

        def unit(u):
            return 2 * (u // 4) + u % 2, (u // 2) % 2

        def lo_on_dve(g):
            return g % SPU in (1, 2)

        def wait_lo(eng, b, g):
            u, s = divmod(g, SPU)
            if lo_on_dve(g):
                wait(eng, s_plo_dve, b, 2 * UNITS, 2 * u + s)
            else:
                wait(eng, s_plo_pool, b, 2 * UNITS, 2 * u + (1 if s == 0 else 2))

        def v_parts(tile, i, j):
            return (tile[:, 4 * j:4 * j + 4, 2 * i:2 * i + 2, 0:D],
                    e32["v"][:, j, :].rearrange("p (c h d) -> p c h d", c=4, h=2))

        def low(eng, kind, i, j, b):
            wait(eng, s_hi[kind], b, 4, 2 * i + j + 1)
            half = slice(j * HALF, (j + 1) * HALF)
            src = e32[kind][:, j, :]
            if kind in "kq":
                hi, lo = kq_hi[kind][:, half], kq_lo[kind][:, half]
            if kind == "v":
                (hi, src), (lo, _) = v_parts(v_hi, i, j), v_parts(v_lo, i, j)
            if kind == "o":
                hi, lo = oT_hi[:, i, half], oT_lo[:, i, half]
            eng.tensor_tensor(lo, src, hi, ALU.subtract).then_inc(s_lo[kind], 1)

        def residual(eng, i, half, b):
            j = i + 2 * half
            wait(eng, s_y, b, 4, j + 1)
            wait(eng, s_xres, b, 16, 16)
            n = slice(half * HALF, (half + 1) * HALF)
            eng.tensor_tensor(y32[:, i, n], y32[:, i, n], xres[:, i, n], ALU.add).then_inc(s_yx, 1)

        @block.sync
        def _(sp):
            sp.sem_inc(s_out, OUT_SEED)
            for t in range(CT):
                sp.dma_start(xin[:, t, :], x_v[0, :, t, :]).then_inc(s_xin[t], 16)
            for n, w in (("v", wv), ("p", wp)):
                sp.dma_start(w_in[n][:, :, :], w.rearrange("(t p) c -> p t c", p=P)).then_inc(s_w[n], 16)

            def image(b):
                return b[1] if b[0] is None else b[0] + b[1]

            def load_next(b, img, tiles=range(CT)):
                for t in tiles:
                    wait(sp, (s_zlo, s_zlo_dve)[t], b, 1, 1)
                    sp.dma_start(xin[:, t, :], x_v[img, :, t, :]).then_inc(s_xin[t], 16)

            def dup(n, p, b, h, signal):
                wait(sp, (s_lo if n == "k" else s_hi)[n], b, 4, 2 * p + 2)
                top, second = (k_both, kq_lo[n]) if n == "k" else (q_twice, kq_hi[n])
                rows = slice(h * D, (h + 1) * D)
                sp.dma_start(top[0:D, 2 * p + h, :], kq_hi[n][rows, :]).then_inc(signal, 16)
                sp.dma_start(top[D:P, 2 * p + h, :], second[rows, :]).then_inc(signal, 16)

            def dup_low(n, p, b, signal):
                wait(sp, s_lo[n], b, 4, 2 * p + 2)
                dst, src = (k_one, kq_hi[n]) if n == "k" else (q_max, kq_lo[n])
                for h in range(2):
                    sp.dma_start(dst[0:D, 2 * p + h, :], src[h * D:(h + 1) * D, :]).then_inc(signal, 16)

            def dup_all(n, p, b):
                for h in range(2):
                    dup(n, p, b, h, s_dup[n])
                dup_low(n, p, b, s_dup[n])

            def shift_to_row(b, u):
                head, half = unit(u)
                wait(sp, s_mx_free, b, MXJ * UNITS, MXJ * (u + 1))
                sp.dma_start(q_max[D:D + 1, head, half * HALF:(half + 1) * HALF],
                             shift_row[:, u % 2, :]).then_inc(s_shift_dma, 16)

            def slot(b, g, prev, nxt, cur):
                u, s = divmod(g, SPU)
                v = shift_at(b, g, nxt, cur)
                if v:
                    shift_to_row(*v)
                if g == 2 and cur:
                    dup_all("k", 1, b)
                if g == 4 and cur:
                    dup_all("q", 1, b)
                if g == 12 and prev:
                    for j in range(4):
                        wait(sp, s_yx, before(b), 4, j + 1)
                        half = slice((j // 2) * HALF, (j // 2 + 1) * HALF)
                        sp.dma_start(out_v[image(before(b)), :, j % 2, half], y32[:, j % 2, half]).then_inc(s_out, 16)
                if g in (15, 19) and nxt:
                    load_next(after(b), (b[0] + 2) % B, [(g - 15) // 4])
                if g == 23 and cur:
                    sp.dma_start(xres[:, :, :], x_v[image(b)]).then_inc(s_xres, 16)
                if g == 19 and nxt:
                    dup_all("k", 0, after(b))
                if g == 22 and nxt:
                    dup_all("q", 0, after(b))

            for n in "kq":
                for h in range(2):
                    dup(n, 0, (None, 0), h, s_first[n][h])
            for n in "kq":
                dup_low(n, 0, (None, 0), s_first_low[n])
            load_next((None, 0), 1)
            for n in "kq":
                for signal in (*s_first[n], s_first_low[n]):
                    sp.wait_ge(signal, 16 * 2)
                sp.sem_inc(s_dup[n], 16 * 6)
            shift_to_row((None, 0), 0)
            batches(sp, slot)
            sp.wait_ge(s_out, 16 * 4 * B + OUT_SEED)

        @block.tensor
        def _(pe):
            latest = Latest()

            def bank_empty():
                if latest.job is None:
                    return
                kind, i, j, b = latest.job
                if kind in SPLIT:
                    wait(pe, s_e32[kind], b, 4, 2 * i + j + 1)
                elif kind == "y":
                    wait(pe, s_y, b, 4, i + 2 * j + 1)
                else:
                    wait(pe, {"mean": s_gmean, "var": s_gvar, "gnb": s_gnb, "gnb_v": s_gnb_v, "wpbv": s_wpbv}[kind],
                         b, 1, 1)

            def parts(dst, lhs, rhs, first=True):
                for t in range(CT):
                    (lh, ll), (rh, rl) = lhs(t), rhs(t)
                    for n, (a, c) in enumerate(((lh, rh), (lh, rl), (ll, rh))):
                        yield nc.tensor.matmul(dst, a, c, start=first and t == 0 and n == 0,
                                               stop=t == CT - 1 and n == 2, skip_group_check=True)

            def job(kind, i, j, b, bank=gen):
                if kind in "kqv":
                    wait(pe, s_zlo, b, 1, 1)
                    wait(pe, s_zlo_dve, b, 1, 1)
                if kind == "mean":
                    wait(pe, s_mv, b, 1, 1)
                if kind == "var":
                    wait(pe, s_dev, b, 1, 1)
                if kind == "o":
                    wait(pe, s_o32, b, UNITS, 4 * i + 2 * j + 2)
                if kind == "y":
                    wait(pe, s_lo["o"], b, 4, 3 + j)
                if bank is gen:
                    bank_empty()
                half = slice(j * HALF, (j + 1) * HALF)
                if kind in "kq":
                    o = slice(i * P, (i + 1) * P)
                    for mm in parts(bank[:, :], lambda t: (w_hi[kind][:, t, o], w_lo[kind][:, t, o]),
                                    lambda t: (z_hi[:, t, half], z_lo[:, t, half])):
                        last = mm
                if kind == "v":
                    o = slice(i * P, (i + 1) * P)
                    for c in range(4):
                        k = slice((4 * j + c) * P, (4 * j + c + 1) * P)
                        for mm in parts(bank[:, c * P:(c + 1) * P], lambda t: (z_hi[:, t, k], z_lo[:, t, k]),
                                        lambda t: (w_hi["v"][:, t, o], w_lo["v"][:, t, o]), first=c == 0):
                            last = mm
                if kind == "y":
                    o = slice(i * P, (i + 1) * P)
                    for mm in parts(bank[:, :], lambda t: (w_hi["p"][:, t, o], w_lo["p"][:, t, o]),
                                    lambda t: (oT_hi[:, t, half], oT_lo[:, t, half])):
                        last = mm
                if kind == "o":
                    for q in range(QT):
                        last = nc.tensor.transpose(bank[:, q * P:(q + 1) * P], o32[:, j, q, :], ident[:, :])
                if kind == "mean":
                    last = nc.tensor.matmul(bank[:, 0:CT], group_avg[:, :], mv[:, :, 0], start=True, stop=True)
                if kind == "var":
                    last = nc.tensor.matmul(bank[:, 0:CT], group_avg[:, :], dev2[:, :], start=True, stop=True)
                last.then_inc(s_gen_full, 1)
                if bank is gen:
                    latest.job = (kind, i, j, b)

            def maximum(b, u, j):
                head, half = unit(u)
                wait(pe, s_mx_free, b, MXJ * UNITS, MXJ * u + j - 1)
                q = half * HALF + (j // 2) * P
                nc.tensor.matmul(mxb[(MXJ * u + j) % 2][:, :], q_twice[:, head, q:q + P],
                                 k_both[:, head, (j % 2) * 512:(j % 2 + 1) * 512],
                                 start=True, stop=True).then_inc(s_mx_full, 1)

            def shift_transpose(b, u):
                j = MXJ - 1
                wait(pe, s_mx_free, b, MXJ * UNITS, MXJ * u + j - 1)
                wait(pe, s_shift, b, UNITS, u + 1)
                nc.tensor.matmul(mxb[(MXJ * u + j) % 2][0:QT, 0:P], shift[:, u % 2, :], ident16[:, :],
                                 start=True, stop=True).then_inc(s_mx_full, 1)

            def scores(b, g):
                u, s = divmod(g, SPU)
                head, half = unit(u)
                q = slice(half * HALF, (half + 1) * HALF)
                if s == 0:
                    wait(pe, s_shift_dma, b, 16 * UNITS, 16 * (u + 1))
                wait(pe, s_exp, b, SLOTS, g - 1)
                for c in range(CPS):
                    k = slice((CPS * s + c) * P, (CPS * s + c + 1) * P)
                    dst = st[g % 2][:, c * HALF:(c + 1) * HALF]
                    nc.tensor.matmul(dst, k_both[:, head, k], q_twice[:, head, q], start=True, stop=False)
                    last = nc.tensor.matmul(dst, k_one[:, head, k], q_max[:, head, q], start=False, stop=True)
                last.then_inc(s_st, 1)

            def weigh(b, g):
                u, s = divmod(g, SPU)
                head, _ = unit(u)
                wait(pe, s_phi, b, SLOTS, g + 1)
                wait_lo(pe, b, g)
                if s == 0:
                    wait(pe, s_o32, b, UNITS, u)
                    if u % 4 == 0:
                        wait(pe, s_lo["v"], b, 4, u // 2 + 2)
                for c in range(CPS):
                    k = CPS * s + c
                    for q in range(QT):
                        qs = slice(q * P, (q + 1) * P)
                        hi, lo = p_hi[:, g % PR, c, qs], p_lo[:, g % PR, c, qs]
                        nc.tensor.matmul(pv_v[:, q, :], hi, v_hi[:, k, head, :], start=k == 0 and q == 0,
                                         stop=False, skip_group_check=True)
                        nc.tensor.matmul(pv_v[:, q, 0:D], hi, v_lo[:, k, head, :], start=False, stop=False,
                                         skip_group_check=True)
                        last = nc.tensor.matmul(pv_v[:, q, :], lo, v_hi[:, k, head, :], start=False,
                                                stop=k == NK - 1, skip_group_check=True)
                last.then_inc(s_pv, 1)

            def slot(b, g, prev, nxt, cur):
                u, s = divmod(g, SPU)
                if cur:
                    scores(b, g)
                done = shift_at(b, g, nxt, cur)
                v, n = maxima_at(b, g, nxt, cur)
                todo = job_at(g, b, prev, nxt, cur)
                old = back(b, g, LAG, prev, cur)
                early = done and long_at(g, b, prev, nxt, cur)
                if early:
                    job(*todo)
                if done:
                    shift_transpose(*done)
                if v:
                    if n == 0 and v[1] % 4 == 0:
                        for kind in "kq":
                            wait(pe, s_dup[kind], v[0], 16 * 12, 16 * 6 * (v[1] // 4 + 1))
                    maximum(*v, n)
                if todo and not early:
                    job(*todo, tail_bank(g, cur))
                if early and old:
                    weigh(*old)
                if v:
                    maximum(*v, n + 1)
                if old and not early:
                    weigh(*old)

            def transpose_weights(m, n):
                pe.wait_ge(s_w[n], 16)
                for t in range(CT):
                    for o in range(CT):
                        last = nc.tensor.transpose(weight_banks[m][:, t * C + o * P:t * C + (o + 1) * P],
                                                   w_in[n][:, o, t * P:(t + 1) * P], ident[:, :])
                last.then_inc(s_wT, 1)

            def times_column(matrices, signal):
                bank_empty()
                for m, (n, column) in enumerate(matrices):
                    for o in range(CT):
                        for t in range(CT):
                            last = nc.tensor.matmul(gen[:, m * CT + o:m * CT + o + 1],
                                                    wT[n][:, t, o * P:(o + 1) * P], column[:, t:t + 1],
                                                    start=m == o == t == 0, stop=t == CT - 1, skip_group_check=True)
                last.then_inc(s_gen_full, 1)
                latest.job = (signal, 0, 0, (None, 0))

            pe.wait_ge(s_const, 3)
            pe.wait_ge(s_vec, 16 * 6)
            nc.tensor.transpose(pv[:, 0:6 * CT], vec_rows[:, :], ident[0:6 * CT, 0:6 * CT]).then_inc(s_vecT, 1)
            job("mean", 0, 0, (None, 0))
            transpose_weights(0, "k")
            job("var", 0, 0, (None, 0))
            transpose_weights(1, "q")
            transpose_weights(2, "v")
            pe.wait_ge(s_wraw, 2)
            pe.wait_ge(s_cols, 1)
            times_column([("k", vec["gn_b"]), ("q", vec["gn_b"])], "gnb")
            transpose_weights(3, "p")
            for n, ((kind, i, j), bank) in enumerate(zip(FIRST_JOBS, first_banks)):
                pe.wait_ge(s_wlo, {"k": 1, "q": 2, "v": 3}[kind])
                if n < 3:
                    pe.wait_ge(s_wraw, max(n + 1, 2))
                    pe.wait_ge(s_wsc, (n + 1) * CT)
                if n >= 4:
                    pe.wait_ge(s_e32["k" if n < 6 else "q"], n % 2 + 1)
                job(kind, i, j, (None, 0), bank)
            times_column([("v", vec["gn_b"])], "gnb_v")
            for n in "kq":
                pe.wait_ge(s_first[n][0], 16 * 2)
            pe.wait_ge(s_wraw, 4)
            pe.wait_ge(s_wsc, 4 * CT)
            for j in range(MXJ - 1):
                maximum((None, 0), 0, j)
            pe.wait_ge(s_bias, 3)
            times_column([("p", bias["v"])], "wpbv")
            shift_transpose((None, 0), 0)
            for n in "kq":
                pe.wait_ge(s_first[n][1], 16 * 2)
            for j in range(4):
                maximum((None, 0), 1, j)
            pe.wait_ge(s_e32["k"], 3)
            pe.wait_ge(s_e32["q"], 3)
            pe.wait_ge(s_e32["v"], 2)
            for n in "kq":
                pe.wait_ge(s_first_low[n], 16 * 2)
            pe.wait_ge(s_ones, 2)
            batches(pe, slot, [latest])

        @block.scalar
        def _(act):
            jobs = Tally(len(JOBS))

            for m, a in enumerate((gn_w, gn_b, bk, bq, bv, bp)):
                act.dma_start(vec_rows[CT * m:CT * (m + 1), :], a.rearrange("(t p) -> t p", p=P)).then_inc(s_vec, 16)
            for n, w in (("k", wk), ("q", wq)):
                act.dma_start(w_in[n][:, :, :], w.rearrange("(t p) c -> p t c", p=P)).then_inc(s_w[n], 16)
            act.wait_ge(s_const, 3)
            nc.scalar.activation(first_use[:, :], eps[:, :], ACT.Exp)

            def job(kind, i, j, b, bank=gen):
                jobs.add()
                act.wait_ge(s_gen_full, jobs.value())
                if kind in SPLIT and not (kind == "o" and i == 0):
                    wait(act, s_lo[kind], b, 4, max(2 * i + j - 1, 0))
                if kind in "kq":
                    last = nc.scalar.activation(e32[kind][:, j, :], bank[:, :], ACT.Identity,
                                                bias=bias_s[kind][:, i:i + 1],
                                                scale=QKV_SCALE / (Z_SCALE * W_SCALE))
                if kind == "v":
                    last = nc.scalar.activation(e32[kind][:, j, :], bank[:, :], ACT.Copy,
                                                scale=QKV_SCALE / (Z_SCALE * W_SCALE))
                if kind == "o":
                    last = nc.scalar.activation(e32[kind][:, j, :], bank[:, :], ACT.Copy, scale=O_SCALE)
                if kind in SPLIT:
                    last.then_inc(s_e32[kind], 1)
                if kind == "y":
                    act.wait_ge(s_bias, 4)
                    wait(act, s_out, b, 64, OUT_SEED)
                    last = nc.scalar.activation(y32[:, i, j * HALF:(j + 1) * HALF], bank[:, :], ACT.Identity,
                                                bias=bias["p"][:, i:i + 1], scale=1.0 / (O_SCALE * W_SCALE))
                    last.then_inc(s_y, 1)
                if kind == "mean":
                    nc.scalar.activation(gmean[:, :], bank[:, 0:CT], ACT.Copy).then_inc(s_gmean, 1)
                if kind == "var":
                    nc.scalar.activation(gvar[:, :], bank[:, 0:CT], ACT.Copy).then_inc(s_gvar, 1)

            def slot(b, g, prev, nxt, cur):
                u, s = divmod(g, SPU)
                if cur:
                    wait(act, s_st, b, SLOTS, g + 1)
                    if g >= SPU or prev:
                        wait_lo(act, *back(b, g, SPU, prev, cur))
                    nc.scalar.activation(p32[:, s, :], st[g % 2][:, :], ACT.Exp, scale=SM_SCALE / M_SCALE)\
                      .then_inc(s_exp, 1)
                    wait(act, s_exp, b, SLOTS, g + 1)
                    wait(act, s_pv, b, SLOTS, g + 1 - PR)
                    nc.scalar.activation(p_hi[:, g % PR, :, :], p32[:, s, :].rearrange("p (c n) -> p c n", n=HALF),
                                         ACT.Copy).then_inc(s_phi, 1)
                todo = job_at(g, b, prev, nxt, cur)
                if todo:
                    job(*todo, tail_bank(g, cur))
                if g in (11, 12) and cur:
                    z_high(after(b), g - 11)

            def z_high(b, t):
                wait(act, s_z32, b, CT, t + 1)
                nc.scalar.activation(z_hi[:, t, :], xin[:, t, :], ACT.Copy).then_inc(s_zhi, 1)

            def from_bank(dst, signal):
                jobs.add()
                act.wait_ge(s_gen_full, jobs.value())
                nc.scalar.activation(dst, gen[:, 0:dst.free_size()], ACT.Copy).then_inc(signal, 1)

            def raw_weights(m, n):
                act.wait_ge(s_wT, m + 1)
                nc.scalar.activation(wT[n][:, :, :], weight_banks[m][:, :].rearrange("p (t o) -> p t o", t=CT),
                                     ACT.Copy).then_inc(s_wraw, 1)

            def split_weights(m, n):
                for t in range(CT):
                    scale = W_SCALE if n == "p" else gam_sc[:, t:t + 1]
                    nc.scalar.activation(w_sc[n][:, t, :], weight_banks[m][:, t * C:(t + 1) * C], ACT.Copy,
                                         scale=scale).then_inc(s_wsc, 1)
                act.wait_ge(s_wsc, CT * (m + 1))
                nc.scalar.activation(w_hi[n][:, :, :], w_sc[n][:, :, :], ACT.Copy).then_inc(s_whi, 1)

            job("mean", 0, 0, (None, 0))
            raw_weights(0, "k")
            job("var", 0, 0, (None, 0))
            raw_weights(1, "q")
            act.wait_ge(s_gam, 1)
            split_weights(0, "k")
            z_high((None, 0), 0)
            z_high((None, 0), 1)
            from_bank(w_gnb[:, 0:2, :].rearrange("p n o -> p (n o)"), s_gnb)
            split_weights(1, "q")
            raw_weights(2, "v")
            split_weights(2, "v")
            raw_weights(3, "p")
            act.wait_ge(s_bias, 2)
            for (kind, i, j), bank in zip(FIRST_JOBS, first_banks):
                job(kind, i, j, (None, 0), bank)
            from_bank(w_gnb[:, 2, :], s_gnb_v)
            split_weights(3, "p")
            from_bank(wp_bv[:, :], s_wpbv)
            batches(act, slot, [jobs])

        @block.vector
        def _(dve):
            def then(ins):
                dve.drain()

            def row_max(b, u, j):
                wait(dve, s_mx_full, b, MXJ * UNITS, MXJ * u + j + 1)
                nc.vector.reduce_max(mx8[:, u % 2, j // 2, j % 2:j % 2 + 1], mxb[(MXJ * u + j) % 2][:, :], AX.X)\
                  .then_inc(s_mx_free, 1)

            def make_shift(b, u):
                wait(dve, s_mx_free, b, MXJ * UNITS, MXJ * u + 2 * QT)
                then(nc.vector.reduce_max(mx4[:, u % 2, :], mx8[:, u % 2, :, :], AX.X))
                nc.vector.tensor_scalar(shift[:, u % 2, :], mx4[:, u % 2, :], -1.0 / M_SCALE, P_LOG / SM_SCALE,
                                        ALU.mult, ALU.add).then_inc(s_shift, 1)

            def row_out(b, u):
                wait(dve, s_mx_full, b, MXJ * UNITS, MXJ * (u + 1))
                wait(dve, s_shift_dma, b, 16 * UNITS, 16 * (u - 1))
                nc.vector.tensor_copy(shift_row[:, u % 2, :], mxb[(MXJ * u + MXJ - 1) % 2][0:QT, 0:P])\
                  .then_inc(s_mx_free, 1)

            def high(kind, i, j, b):
                wait(dve, s_e32[kind], b, 4, 2 * i + j + 1)
                half = slice(j * HALF, (j + 1) * HALF)
                src = e32[kind][:, j, :]
                if kind in "kq":
                    wait(dve, s_dup[kind], b, 16 * 12, 16 * 6 * i)
                    dst = kq_hi[kind][:, half]
                if kind == "v":
                    dst, src = v_parts(v_hi, i, j)
                if kind == "o":
                    dst = oT_hi[:, i, half]
                nc.vector.tensor_copy(dst, src).then_inc(s_hi[kind], 1)

            def normalise(b, u):
                head, half = unit(u)
                wait(dve, s_pv, b, SLOTS, SPU * (u + 1))
                then(nc.vector.reciprocal(rden[:, u % 2, :], pv_v[:, :, D]))
                nc.vector.tensor_tensor(o32[:, half, :, (u % 2) * D:(u % 2 + 1) * D], pv_v[:, :, 0:D],
                                        rden[:, u % 2, :].unsqueeze(2).to_broadcast([P, QT, D]), ALU.mult)\
                  .then_inc(s_o32, 1)

            def channel_stats(b, t):
                wait(dve, s_xin[t], b, 16, 16)
                for n in range(2):
                    then(nc.vector.bn_stats(bn[:, t, n, :], xin[:, t, n * 512:(n + 1) * 512]))
                ins = nc.vector.bn_aggr(mv[:, t, :], bn[:, t, :, :].rearrange("p n s -> p (n s)"))
                if t == CT - 1:
                    ins.then_inc(s_mv, 1)

            def about_group_mean(b):
                wait(dve, s_gmean, b, 1, 1)
                wait(dve, s_mv, b, 1, 1)
                then(nc.vector.tensor_tensor(dev[:, :], mv[:, :, 0], gmean[:, :], ALU.subtract))
                then(nc.vector.tensor_tensor(dev[:, :], dev[:, :], dev[:, :], ALU.mult))
                nc.vector.tensor_tensor(dev2[:, :], dev[:, :], mv[:, :, 1], ALU.add).then_inc(s_dev, 1)

            def z_of(b, t):
                wait(dve, s_za, b, 1, 1)
                nc.vector.tensor_scalar(xin[:, t, :], xin[:, t, :], gmean[:, t:t + 1], z_a[:, t:t + 1],
                                        ALU.subtract, ALU.mult).then_inc(s_z32, 1)

            def z_low_dve(b):
                wait(dve, s_zhi, b, CT, CT)
                nc.vector.tensor_tensor(z_lo[:, CT - 1, :], xin[:, CT - 1, :], z_hi[:, CT - 1, :], ALU.subtract)\
                  .then_inc(s_zlo_dve, 1)

            def slot(b, g, prev, nxt, cur):
                s = g % SPU
                old = back(b, g, LAG + 1, prev, cur)
                if old and old[1] % SPU == SPU - 1:
                    normalise(old[0], old[1] // SPU)
                done = shift_at(b, g, nxt, cur)
                v, n = maxima_at(b, g, nxt, cur)
                long = long_at(g, b, prev, nxt, cur)
                if not (done and long):
                    if done:
                        row_out(*done)
                    if v:
                        row_max(*v, n)
                        if s >= 2 and not long:
                            row_max(*v, n + 1)
                todo = job_at(g - 1, b, prev, nxt, cur)
                if todo and todo[0] in SPLIT:
                    high(*todo)
                    if not cur:
                        low(dve, *todo)
                if todo and todo[0] == "y" and not cur:
                    residual(dve, *todo[1:])
                old = back(b, g, 1, prev, cur)
                if old and lo_on_dve(old[1]):
                    wait(dve, s_phi, old[0], SLOTS, old[1] + 1)
                    nc.vector.tensor_tensor(p_lo[:, old[1] % PR, :, :],
                                            p32[:, old[1] % SPU, :].rearrange("p (c n) -> p c n", n=HALF),
                                            p_hi[:, old[1] % PR, :, :], ALU.subtract).then_inc(s_plo_dve, 1)
                if done and long:
                    row_out(*done)
                    if v:
                        row_max(*v, n)
                if v and (s < 2 or long):
                    row_max(*v, n + 1)
                if v and n == 2 * QT - 2:
                    make_shift(*v)
                if g in (0, 2) and cur:
                    channel_stats(after(b), g // 2)
                if g == 5 and cur:
                    about_group_mean(after(b))
                if g in (8, 9) and cur:
                    z_of(after(b), g - 8)
                if g == 13 and nxt:
                    z_low_dve(after(b))

            nc.vector.memset(v_hi[:, :, :, D], QKV_SCALE).then_inc(s_ones, 1)
            for t in range(CT):
                channel_stats((None, 0), t)
            dve.wait_ge(s_vecT, 1)
            nc.vector.tensor_copy(vec_cols[:, :], pv[:, 0:6 * CT]).then_inc(s_cols, 1)
            dve.wait_ge(s_cols, 1)
            nc.vector.tensor_scalar(gam_sc[:, :], vec["gn_w"], W_SCALE, None, ALU.mult).then_inc(s_gam, 1)
            about_group_mean((None, 0))
            for t in range(CT):
                z_of((None, 0), t)
            z_low_dve((None, 0))
            dve.wait_ge(s_gnb, 1)
            for m, n in enumerate("kq"):
                then(nc.vector.tensor_tensor(bias[n][:, :], w_gnb[:, m, :], vec[n], ALU.add))
                nc.vector.tensor_scalar(bias_s[n][:, :], bias[n][:, :], QKV_SCALE, None, ALU.mult)\
                  .then_inc(s_bias, 1)
            for kind, i, j in FIRST_JOBS[:4]:
                high(kind, i, j, (None, 0))
                low(dve, kind, i, j, (None, 0))
            dve.wait_ge(s_gnb_v, 1)
            nc.vector.tensor_tensor(bias["v"][:, :], w_gnb[:, 2, :], vec["v"], ALU.add).then_inc(s_bias, 1)
            for j in range(MXJ - 1):
                row_max((None, 0), 0, j)
            make_shift((None, 0), 0)
            row_out((None, 0), 0)
            for j in range(4):
                row_max((None, 0), 1, j)
            for todo in FIRST_JOBS[4:]:
                high(*todo, (None, 0))
            dve.wait_ge(s_wpbv, 1)
            nc.vector.tensor_tensor(bias["p"][:, :], wp_bv[:, :], vec["p"], ALU.add).then_inc(s_bias, 1)
            batches(dve, slot)

        @block.gpsimd
        def _(pool):
            def then(ins):
                pool.drain()

            def norm_factors(b):
                wait(pool, s_gvar, b, 1, 1)
                then(nc.gpsimd.tensor_tensor(veps[:, :], gvar[:, :], eps[:, :], ALU.add))
                then(nc.gpsimd.tensor_tensor(rstd[:, :], veps[:, :], expo[:, :], ALU.pow))
                then(nc.gpsimd.tensor_tensor(z_a[:, :], rstd[:, :], rstd[:, :], ALU.mult))
                then(nc.gpsimd.tensor_tensor(z_a[:, :], z_a[:, :], veps[:, :], ALU.mult))
                then(nc.gpsimd.tensor_scalar(z_a[:, :], z_a[:, :], -0.5 * Z_SCALE, 1.5 * Z_SCALE, ALU.mult, ALU.add))
                nc.gpsimd.tensor_tensor(z_a[:, :], z_a[:, :], rstd[:, :], ALU.mult).then_inc(s_za, 1)

            def z_low(b):
                wait(pool, s_zhi, b, CT, 1)
                nc.gpsimd.tensor_tensor(z_lo[:, 0, :], xin[:, 0, :], z_hi[:, 0, :], ALU.subtract).then_inc(s_zlo, 1)

            def slot(b, g, prev, nxt, cur):
                todo = job_at(g - 1, b, prev, nxt, cur)
                if todo and todo[0] in SPLIT and cur:
                    low(pool, *todo)
                old = back(b, g, 1, prev, cur)
                if old and not lo_on_dve(old[1]):
                    wait(pool, s_phi, old[0], SLOTS, old[1] + 1)
                    nc.gpsimd.tensor_tensor(p_lo[:, old[1] % PR, :, :],
                                            p32[:, old[1] % SPU, :].rearrange("p (c n) -> p c n", n=HALF),
                                            p_hi[:, old[1] % PR, :, :], ALU.subtract).then_inc(s_plo_pool, 1)
                if todo and todo[0] == "y" and cur:
                    residual(pool, *todo[1:])
                if g == 7 and cur:
                    norm_factors(after(b))
                if g == 12 and cur:
                    z_low(after(b))

            nc.gpsimd.memset(ident[:, :], 0.0).then_inc(s_cfill, 1)
            nc.gpsimd.memset(ident16[:, :], 0.0).then_inc(s_cfill, 1)
            nc.gpsimd.memset(group_avg[:, :], 1.0 / GROUP).then_inc(s_cfill, 1)
            nc.gpsimd.memset(expo[:, :], -0.5).then_inc(s_cfill, 1)
            nc.gpsimd.memset(eps[:, :], EPS).then_inc(s_cfill, 1)
            pool.wait_ge(s_cfill, 5)
            for m in (ident, ident16):
                nc.gpsimd.affine_select(out=m[:, :], in_=m[:, :], compare_op=ALU.not_equal, fill=1.0, base=0,
                                        pattern=[[-1, P]], channel_multiplier=1).then_inc(s_const, 1)
            blocks = group_avg[:, :].rearrange("p (g n) -> p g n", n=GROUP)
            then(nc.gpsimd.affine_select(out=blocks, in_=blocks, compare_op=ALU.is_ge, fill=0.0, base=0,
                                         pattern=[[-GROUP, P // GROUP], [0, GROUP]], channel_multiplier=1))
            nc.gpsimd.affine_select(out=blocks, in_=blocks, compare_op=ALU.is_ge, fill=0.0, base=GROUP - 1,
                                    pattern=[[GROUP, P // GROUP], [0, GROUP]], channel_multiplier=-1)\
              .then_inc(s_const, 1)
            pool.drain()
            nc.gpsimd.memset(k_one[D:D + 1, :, :], M_SCALE).then_inc(s_ones, 1)
            pool.drain()
            def low_weights(m, n):
                pool.wait_ge(s_whi, m + 1)
                nc.gpsimd.tensor_tensor(w_lo[n][:, :, :], w_sc[n][:, :, :], w_hi[n][:, :, :], ALU.subtract)\
                  .then_inc(s_wlo, 1)

            norm_factors((None, 0))
            low_weights(0, "k")
            z_low((None, 0))
            low_weights(1, "q")
            low_weights(2, "v")
            low_weights(3, "p")
            for todo in FIRST_JOBS[4:]:
                low(pool, *todo, (None, 0))
            batches(pool, slot)


_INS = ["x", "L0_conv_gn_w", "L0_conv_gn_b", "L0_conv_wq", "L0_conv_bq", "L0_conv_wk", "L0_conv_bk",
        "L0_conv_wv", "L0_conv_bv", "L0_conv_wp", "L0_conv_bp"]


def kernel(**inputs):
    import numpy as _np
    import concourse.bacc as _bacc
    from concourse import mybir as _mybir
    from concourse.bass_utils import run_bass_kernel_spmd as _run

    nc = _bacc.Bacc("TRN2", target_bir_lowering=False, num_devices=1)
    arrays, args = {}, []
    for name in _INS:
        a = _np.ascontiguousarray(inputs[name])
        arrays[f"in_{name}_dram"] = a
        args.append(nc.dram_tensor(f"in_{name}_dram", a.shape, _mybir.dt.from_np(a.dtype), kind="ExternalInput").ap())
    shape = inputs["x"].shape
    args.append(nc.dram_tensor("out_0_dram", shape, _mybir.dt.float32, kind="ExternalOutput").ap())
    attention_block(nc, *args)
    r = _run(nc, [arrays], core_ids=[0])
    return r.results[0]["out_0_dram"]
```
